# Optimizing a Trainium2 kernel written in Bass

```python
import numpy as np
import jax
import jax.numpy as jnp

def _softmax(x, axis=-1):
    return jax.nn.softmax(x, axis=axis)

def _gelu(x):
    return jax.nn.gelu(x, approximate=True)

def _silu(x):
    return jax.nn.silu(x)

def _sigmoid(x):
    return jax.nn.sigmoid(x)

def _layernorm(x, axis=-1, eps=1e-05):
    m = jnp.mean(x, axis=axis, keepdims=True)
    v = jnp.var(x, axis=axis, keepdims=True)
    return (x - m) / jnp.sqrt(v + eps)

def _scatter_add(tgt, idx, src, axis=0):
    return tgt.at[idx].add(src)

def _segment_sum(src, seg, n):
    return jax.ops.segment_sum(src, seg, n)
kernel_name = 'mk_xattn_seq_d1_seqx_r2_14386f'

def setup_inputs(seed: int=0):
    np.random.seed(seed)
    _w = jnp.asarray

    def _rec_inputs():
        import jax
        import jax.numpy as jnp
        _rk = jax.random.key(seed)
        x = 7.22e-05 + 1 * jax.random.normal(jax.random.fold_in(_rk, 1), (16, 256, 512), jnp.float32)
        _lenS = 256 - jax.random.randint(jax.random.fold_in(_rk, 7), (16,), 0, max(1, 256 // 4) + 1, jnp.int32)
        _lenS2 = 256 - jax.random.randint(jax.random.fold_in(_rk, 8), (16,), 0, max(1, 256 // 4) + 1, jnp.int32)
        _ctx_512P = jax.random.normal(jax.random.fold_in(_rk, 11), (16, 16, 256), jnp.float32)
        _ctx_512c = jax.random.dirichlet(jax.random.fold_in(_rk, 511), 0.3 * jnp.ones((16,), jnp.float32), (16, 256))
        _ctx_512t = jnp.einsum('bsk,bkd->bsd', _ctx_512c, _ctx_512P)
        _ctx_512t = _ctx_512t * jax.lax.rsqrt(jnp.mean(jnp.square(_ctx_512t)) + 1e-12) * 0.953939
        ctx_512 = 4.13588e-05 + 0.999923 * (_ctx_512t + 0.3 * jax.random.normal(jax.random.fold_in(_rk, 611), (16, 256, 256), jnp.float32))
        fside_BxSxS_0 = 0.000376506 + 0.999991 * jax.random.normal(jax.random.fold_in(_rk, 12), (16, 256, 256), jnp.float32)
        return (x, ctx_512, fside_BxSxS_0)
    x, ctx_512, fside_BxSxS_0 = _rec_inputs()

    def _L0_xattn_setup():
        import jax, jax.numpy as jnp
        import numpy as np
        EPS = 1e-05

        def _ln(x, g, b):
            mu = jnp.mean(x, axis=-1, keepdims=True)
            var = jnp.var(x, axis=-1, keepdims=True)
            return (x - mu) * jax.lax.rsqrt(var + EPS) * g + b

        def _cma(x1, x2, ln1_g, ln1_b, ln2_g, ln2_b, Wq, bq, Wk, bk, Wv, bv, Wo, bo):
            e = Wq.shape[1]
            scale = e ** (-0.5)
            x1n = _ln(x1, ln1_g, ln1_b)
            x2n = _ln(x2, ln2_g, ln2_b)
            q = x1n @ Wq + bq
            k = x2n @ Wk + bk
            v = x2n @ Wv + bv
            attn = jax.nn.softmax(jnp.einsum('bqe,bke->bqk', q, k) * scale, axis=-1)
            ctx = jnp.einsum('bqk,bke->bqe', attn, v)
            return ctx @ Wo + bo
        key = jax.random.key(seed)
        ks = jax.random.split(key, 24)
        B, Lt, La, Lv = (16, 256, 512, 256)
        Dt, Da, Dv, E = (512, 256, 256, 512)
        s = lambda k, *sh: jax.random.normal(k, sh, dtype=jnp.float32) * 0.02
        inp = {'text': jax.random.normal(ks[0], (B, Lt, Dt), dtype=jnp.float32), 'audio': jax.random.normal(ks[1], (B, La, Da), dtype=jnp.float32), 'video': jax.random.normal(ks[2], (B, Lv, Dv), dtype=jnp.float32), 'a_ln1_g': jnp.ones((Dt,)), 'a_ln1_b': jnp.zeros((Dt,)), 'a_ln2_g': jnp.ones((Da,)), 'a_ln2_b': jnp.zeros((Da,)), 'a_Wq': s(ks[3], Dt, E), 'a_bq': jnp.zeros((E,)), 'a_Wk': s(ks[4], Da, E), 'a_bk': jnp.zeros((E,)), 'a_Wv': s(ks[5], Da, E), 'a_bv': jnp.zeros((E,)), 'a_Wo': s(ks[6], E, Dt), 'a_bo': jnp.zeros((Dt,)), 'v_ln1_g': jnp.ones((Dt,)), 'v_ln1_b': jnp.zeros((Dt,)), 'v_ln2_g': jnp.ones((Dv,)), 'v_ln2_b': jnp.zeros((Dv,)), 'v_Wq': s(ks[7], Dt, E), 'v_bq': jnp.zeros((E,)), 'v_Wk': s(ks[8], Dv, E), 'v_bk': jnp.zeros((E,)), 'v_Wv': s(ks[9], Dv, E), 'v_bv': jnp.zeros((E,)), 'v_Wo': s(ks[10], E, Dt), 'v_bo': jnp.zeros((Dt,)), 'ln_g': jnp.ones((Dt,)), 'ln_b': jnp.zeros((Dt,)), 'fc_W': s(ks[11], Dt, Dt), 'fc_b': jnp.zeros((Dt,))}
        return inp
    _L0_xattn_all = _L0_xattn_setup()
    _L0_xattn_in = {k: v for k, v in _L0_xattn_all.items() if k in ('a_ln1_g', 'a_ln1_b', 'a_ln2_g', 'a_ln2_b', 'a_Wq', 'a_bq', 'a_Wk', 'a_bk', 'a_Wv', 'a_bv', 'a_Wo', 'a_bo', 'v_ln1_g', 'v_ln1_b', 'v_ln2_g', 'v_ln2_b', 'v_Wq', 'v_bq', 'v_Wk', 'v_bk', 'v_Wv', 'v_bv', 'v_Wo', 'v_bo', 'ln_g', 'ln_b', 'fc_W', 'fc_b')}
    del _L0_xattn_all
    return {'x': x, 'ctx_512': ctx_512, 'fside_BxSxS_0': fside_BxSxS_0, 'L0_xattn_a_ln1_g': _L0_xattn_in['a_ln1_g'], 'L0_xattn_a_ln1_b': _L0_xattn_in['a_ln1_b'], 'L0_xattn_a_ln2_g': _L0_xattn_in['a_ln2_g'], 'L0_xattn_a_ln2_b': _L0_xattn_in['a_ln2_b'], 'L0_xattn_a_Wq': _L0_xattn_in['a_Wq'], 'L0_xattn_a_bq': _L0_xattn_in['a_bq'], 'L0_xattn_a_Wk': _L0_xattn_in['a_Wk'], 'L0_xattn_a_bk': _L0_xattn_in['a_bk'], 'L0_xattn_a_Wv': _L0_xattn_in['a_Wv'], 'L0_xattn_a_bv': _L0_xattn_in['a_bv'], 'L0_xattn_a_Wo': _L0_xattn_in['a_Wo'], 'L0_xattn_a_bo': _L0_xattn_in['a_bo'], 'L0_xattn_v_ln1_g': _L0_xattn_in['v_ln1_g'], 'L0_xattn_v_ln1_b': _L0_xattn_in['v_ln1_b'], 'L0_xattn_v_ln2_g': _L0_xattn_in['v_ln2_g'], 'L0_xattn_v_ln2_b': _L0_xattn_in['v_ln2_b'], 'L0_xattn_v_Wq': _L0_xattn_in['v_Wq'], 'L0_xattn_v_bq': _L0_xattn_in['v_bq'], 'L0_xattn_v_Wk': _L0_xattn_in['v_Wk'], 'L0_xattn_v_bk': _L0_xattn_in['v_bk'], 'L0_xattn_v_Wv': _L0_xattn_in['v_Wv'], 'L0_xattn_v_bv': _L0_xattn_in['v_bv'], 'L0_xattn_v_Wo': _L0_xattn_in['v_Wo'], 'L0_xattn_v_bo': _L0_xattn_in['v_bo'], 'L0_xattn_ln_g': _L0_xattn_in['ln_g'], 'L0_xattn_ln_b': _L0_xattn_in['ln_b'], 'L0_xattn_fc_W': _L0_xattn_in['fc_W'], 'L0_xattn_fc_b': _L0_xattn_in['fc_b']}

def reference(x, ctx_512, fside_BxSxS_0, L0_xattn_a_ln1_g, L0_xattn_a_ln1_b, L0_xattn_a_ln2_g, L0_xattn_a_ln2_b, L0_xattn_a_Wq, L0_xattn_a_bq, L0_xattn_a_Wk, L0_xattn_a_bk, L0_xattn_a_Wv, L0_xattn_a_bv, L0_xattn_a_Wo, L0_xattn_a_bo, L0_xattn_v_ln1_g, L0_xattn_v_ln1_b, L0_xattn_v_ln2_g, L0_xattn_v_ln2_b, L0_xattn_v_Wq, L0_xattn_v_bq, L0_xattn_v_Wk, L0_xattn_v_bk, L0_xattn_v_Wv, L0_xattn_v_bv, L0_xattn_v_Wo, L0_xattn_v_bo, L0_xattn_ln_g, L0_xattn_ln_b, L0_xattn_fc_W, L0_xattn_fc_b):
    import jax
    import jax.numpy as jnp

    def _L0_xattn_ref(text, audio, video, a_ln1_g, a_ln1_b, a_ln2_g, a_ln2_b, a_Wq, a_bq, a_Wk, a_bk, a_Wv, a_bv, a_Wo, a_bo, v_ln1_g, v_ln1_b, v_ln2_g, v_ln2_b, v_Wq, v_bq, v_Wk, v_bk, v_Wv, v_bv, v_Wo, v_bo, ln_g, ln_b, fc_W, fc_b):
        import jax, jax.numpy as jnp
        import numpy as np
        EPS = 1e-05

        def _ln(x, g, b):
            mu = jnp.mean(x, axis=-1, keepdims=True)
            var = jnp.var(x, axis=-1, keepdims=True)
            return (x - mu) * jax.lax.rsqrt(var + EPS) * g + b

        def _cma(x1, x2, ln1_g, ln1_b, ln2_g, ln2_b, Wq, bq, Wk, bk, Wv, bv, Wo, bo):
            e = Wq.shape[1]
            scale = e ** (-0.5)
            x1n = _ln(x1, ln1_g, ln1_b)
            x2n = _ln(x2, ln2_g, ln2_b)
            q = x1n @ Wq + bq
            k = x2n @ Wk + bk
            v = x2n @ Wv + bv
            attn = jax.nn.softmax(jnp.einsum('bqe,bke->bqk', q, k) * scale, axis=-1)
            ctx = jnp.einsum('bqk,bke->bqe', attn, v)
            return ctx @ Wo + bo
        out_a = _cma(text, audio, a_ln1_g, a_ln1_b, a_ln2_g, a_ln2_b, a_Wq, a_bq, a_Wk, a_bk, a_Wv, a_bv, a_Wo, a_bo)
        out_v = _cma(text, video, v_ln1_g, v_ln1_b, v_ln2_g, v_ln2_b, v_Wq, v_bq, v_Wk, v_bk, v_Wv, v_bv, v_Wo, v_bo)
        output = out_a + out_v + text
        residual = output
        output = _ln(output, ln_g, ln_b) @ fc_W + fc_b
        return output + residual
    x = _L0_xattn_ref(x, ctx_512, fside_BxSxS_0, L0_xattn_a_ln1_g, L0_xattn_a_ln1_b, L0_xattn_a_ln2_g, L0_xattn_a_ln2_b, L0_xattn_a_Wq, L0_xattn_a_bq, L0_xattn_a_Wk, L0_xattn_a_bk, L0_xattn_a_Wv, L0_xattn_a_bv, L0_xattn_a_Wo, L0_xattn_a_bo, L0_xattn_v_ln1_g, L0_xattn_v_ln1_b, L0_xattn_v_ln2_g, L0_xattn_v_ln2_b, L0_xattn_v_Wq, L0_xattn_v_bq, L0_xattn_v_Wk, L0_xattn_v_bk, L0_xattn_v_Wv, L0_xattn_v_bv, L0_xattn_v_Wo, L0_xattn_v_bo, L0_xattn_ln_g, L0_xattn_ln_b, L0_xattn_fc_W, L0_xattn_fc_b)
    return x

_drawn_inputs = setup_inputs


def setup_inputs(seed=0):
    import zlib

    import numpy as np

    out = dict(_drawn_inputs(seed))
    spreads = {'L0_xattn_a_ln1_g': (1.0, 0.6),
     'L0_xattn_a_ln1_b': (0.0, 0.8),
     'L0_xattn_a_ln2_g': (1.0, 0.6),
     'L0_xattn_a_ln2_b': (0.0, 0.564),
     'L0_xattn_a_bq': (0.0, 0.8),
     'L0_xattn_a_bk': (0.0, 0.8),
     'L0_xattn_a_bv': (0.0, 0.1),
     'L0_xattn_a_bo': (0.0, 0.1),
     'L0_xattn_v_ln1_g': (1.0, 0.6),
     'L0_xattn_v_ln1_b': (0.0, 0.8),
     'L0_xattn_v_ln2_g': (1.0, 0.6),
     'L0_xattn_v_ln2_b': (0.0, 0.585),
     'L0_xattn_v_bq': (0.0, 0.8),
     'L0_xattn_v_bk': (0.0, 0.8),
     'L0_xattn_v_bv': (0.0, 0.1),
     'L0_xattn_v_bo': (0.0, 0.1),
     'L0_xattn_ln_g': (1.0, 0.2),
     'L0_xattn_ln_b': (0.0, 0.1),
     'L0_xattn_fc_b': (0.0, 0.1)}
    factors = {'fside_BxSxS_0': 6.219,
     'L0_xattn_a_Wq': 8.0,
     'L0_xattn_a_Wk': 8.0,
     'L0_xattn_v_Wq': 8.0,
     'L0_xattn_v_Wk': 8.0,
     'L0_xattn_v_Wv': 3.427}
    for name, (base, spread) in spreads.items():
        noise = np.random.default_rng([zlib.crc32(name.encode()), seed]).standard_normal(out[name].shape)
        drawn = base * np.exp(spread * noise) if base else spread * noise
        out[name] = jnp.asarray(drawn.astype(out[name].dtype))
    for name, factor in factors.items():
        out[name] = (out[name] * factor).astype(out[name].dtype)
    return out
```

```python
from contextlib import ExitStack

import concourse.bass as bass
from concourse import mybir

F32 = mybir.dt.float32
F32R = mybir.dt.float32r
ALU = mybir.AluOpType
ACT = mybir.ActivationFunctionType
AX_X = mybir.AxisListType.X
P = 128
EPS = 1e-5


def build(nc, a):
    B, S, D = a["x"].shape
    D2 = a["ctx_512"].shape[2]
    E = a["L0_xattn_a_Wq"].shape[1]
    MODS = ("a", "v")
    DC, EC, D2C = D // P, E // P, D2 // P
    T = S // P
    TILES = 2 * T
    PAIRS = B // 2
    ROWS = TILES * P
    SCALE = float(E) ** -0.5
    assert T == 2 and D2C == 2 and DC == 4 and EC == 4 and D == 512 and S == 256

    x_rows = a["x"].rearrange("(i b) (p t) d -> i p b (t d)", b=2, t=T)
    out_rows = a["out"].rearrange("(i b) (p t) d -> i p b (t d)", b=2, t=T)
    ctx_rows = [a[n].rearrange("(i b) (p t) d -> i p b (t d)", b=2, t=T)
                for n in ("ctx_512", "fside_BxSxS_0")]

    def par(m, name):
        return a[f"L0_xattn_{MODS[m]}_{name}"]

    ctx = ExitStack()
    with ctx:
        def sb(name, shape, dt=F32, stack=ctx):
            return stack.enter_context(nc.sbuf_tensor(name, shape, dt))

        def sem(name):
            return ctx.enter_context(nc.semaphore(name))

        prod = [ctx.enter_context(nc.psum_tensor(f"prod{k}", [P, 512], F32)) for k in range(4)]
        turn = [ctx.enter_context(nc.psum_tensor(f"turn{k}", [P, 512], F32)) for k in range(4)]

        M_hi = sb("M_hi", [P, 2, DC, D2], F32R)
        M_lo = sb("M_lo", [P, 2, DC, D2], F32R)
        WA_hi = sb("WA_hi", [P, 2, D2C, D], F32R)
        WA_lo = sb("WA_lo", [P, 2, D2C, D], F32R)
        fc_hi = sb("fc_hi", [P, DC, D], F32R)
        fc_lo = sb("fc_lo", [P, DC, D], F32R)
        c_row = sb("c_row", [P, D])
        f_row = sb("f_row", [P, D])
        ident = sb("ident", [P, P])
        u_col = sb("u_col", [P, 2, D2C])
        w_hi = sb("w_hi", [P, DC, 2], F32R)
        w_lo = sb("w_lo", [P, DC, 2], F32R)
        r0 = sb("r0", [P, TILES, 2])
        minus_half = sb("minus_half", [P, TILES])
        eps = sb("eps", [P, TILES])

        x_bn = sb("x_bn", [P, TILES, 6])
        x_mv = sb("x_mv", [P, TILES, 2])
        x_ve = sb("x_ve", [P, TILES])
        x_rstd = sb("x_rstd", [P, TILES])
        ctx_bn = sb("ctx_bn", [P, 2, TILES, 6])
        ctx_mv = sb("ctx_mv", [P, 2, TILES, 2])
        ctx_ve = sb("ctx_ve", [P, 2, TILES])
        ctx_rstd = sb("ctx_rstd", [P, 2, TILES])
        y_bn = sb("y_bn", [P, TILES, 6])
        y_mv = sb("y_mv", [P, TILES, 2])
        y_ve = sb("y_ve", [P, TILES])
        y_rstd = sb("y_rstd", [P, TILES])
        r_sb = sb("r_sb", [P, TILES, 2])
        neg_max = sb("neg_max", [P, 2, 2, T])
        neg_top = sb("neg_top", [P, 2, 2, T])
        exp_bias = sb("exp_bias", [P, 2, 2, T])
        exp_sum = sb("exp_sum", [P, 2, 2, T])
        exp_inv = sb("exp_inv", [P, 2, 2, T])

        x_in = sb("x_in", [P, TILES, D])
        x_res = sb("x_res", [P, TILES, D])
        z1 = sb("z1", [P, TILES, D])
        z2 = sb("z2", [P, 2, TILES, D2])
        probs = sb("probs", [P, 2, 2, T, S])
        y = sb("y", [P, TILES, D])
        yn = sb("yn", [P, TILES, D])

        early = ExitStack()
        Wq = [sb(f"Wq{m}", [P, DC, E], stack=early) for m in (0, 1)]
        WqT = [sb(f"WqT{m}", [P, EC, D], stack=early) for m in (0, 1)]
        Wk = [sb(f"Wk{m}", [P, D2C, E], stack=early) for m in (0, 1)]
        WkT = [sb(f"WkT{m}", [P, EC, D2], stack=early) for m in (0, 1)]
        Wv = [sb(f"Wv{m}", [P, D2C, E], stack=early) for m in (0, 1)]
        WvT = [sb(f"WvT{m}", [P, EC, D2], stack=early) for m in (0, 1)]
        Wo = [sb(f"Wo{m}", [P, EC, D], stack=early) for m in (0, 1)]
        Wkg = [probs[:, m, :, :, :].rearrange("p m t s -> p (m t s)").rearrange("p (c e) -> p c e", c=D2C) for m in (0, 1)]
        fcW = y
        bo = sb("bo", [P, 2, D], stack=early)
        fcb = sb("fcb", [P, D], stack=early)
        ones = sb("ones", [P, P], stack=early)
        rep = yn[:].rearrange("p n d -> p (n d)").rearrange("p (k m e q) -> p k m e q", k=2, m=2, e=EC)
        ln_b_rep = sb("ln_b_rep", [P, DC, P], stack=early)
        vec_rows = sb("vec_rows", [64, P], stack=early)
        vec = sb("vec", [P, 64], stack=early)
        cols = sb("cols", [P, 64], stack=early)
        early.close()

        z2r_hi = sb("z2r_hi", [P, 2, TILES, D2], F32R)
        z2r_lo = sb("z2r_lo", [P, 2, TILES, D2], F32R)
        z1T_hi = sb("z1T_hi", [P, DC, ROWS], F32R)
        z1T_lo = sb("z1T_lo", [P, DC, ROWS], F32R)
        z2T_hi = sb("z2T_hi", [P, 2, D2C, ROWS], F32R)
        z2T_lo = sb("z2T_lo", [P, 2, D2C, ROWS], F32R)
        tT_hi = sb("tT_hi", [P, 2, D2C, ROWS], F32R)
        tT_lo = sb("tT_lo", [P, 2, D2C, ROWS], F32R)
        cT_hi = sb("cT_hi", [P, 2, 2, D2C, S], F32R)
        cT_lo = sb("cT_lo", [P, 2, 2, D2C, S], F32R)
        share_hi = sb("share_hi", [P, 4, 512], F32R)
        share_lo = sb("share_lo", [P, 4, 512], F32R)

        vec_at, n = {}, 0
        for m in (0, 1):
            for name, c in (("ln1_g", DC), ("ln1_b", DC), ("ln2_g", D2C), ("ln2_b", D2C),
                            ("bq", EC), ("bk", EC), ("bv", EC)):
                vec_at[m, name] = (n, c)
                n += c
        for name in ("ln_g", "ln_b"):
            vec_at[name] = (n, DC)
            n += DC
        NVEC = n

        def v_(m, name, k):
            at = vec_at[m, name][0] + k
            return vec[:, at:at + 1]

        def col(kind, m, k0, k1):
            at = (kind * 2 + m) * 4
            return cols[:, at + k0:at + k1]

        BQ, BK, BV, G1S = range(4)

        s_vec = sem("s_vec")
        s_w = {k: sem("s_" + k) for k in ("Wq0", "Wq1", "Wk0", "Wk1", "Wv0", "Wv1", "Wo0", "Wo1", "fc", "rows")}
        s_ident = sem("s_ident")
        s_ident0 = sem("s_ident0")
        s_const = sem("s_const")
        s_vecT = sem("s_vecT")
        s_vec_sb = sem("s_vec_sb")
        s_g = sem("s_g")
        s_pw = sem("s_pw")
        s_ew = sem("s_ew")
        s_bp = sem("s_bp")
        s_bc = sem("s_bc")
        s_up = sem("s_up")
        s_uc = sem("s_uc")
        s_rep = sem("s_rep")
        s_big = sem("s_big")
        s_big_hi = sem("s_big_hi")
        s_big_lo = sem("s_big_lo")
        s_row = sem("s_row")
        s_row_sb = sem("s_row_sb")
        s_bo = sem("s_bo")
        s_fc_hi = sem("s_fc_hi")
        s_fc_lo = sem("s_fc_lo")
        s_r0 = sem("s_r0")
        s_wc = sem("s_wc")

        x_loaded = sem("x_loaded")
        ctx_loaded = [sem("ctxa_loaded"), sem("ctxv_loaded")]
        res_loaded = sem("res_loaded")
        stored = [sem("stored0"), sem("stored1")]
        x_bn_done = sem("x_bn_done")
        x_stats = sem("x_stats")
        x_ve_done = sem("x_ve_done")
        x_rstd_done = sem("x_rstd_done")
        z1_ready = sem("z1_ready")
        ctx_bn_done = sem("ctx_bn_done")
        ctx_stats = sem("ctx_stats")
        ctx_ve_done = sem("ctx_ve_done")
        ctx_rstd_done = sem("ctx_rstd_done")
        z2_ready = sem("z2_ready")
        z2r_hi_done = sem("z2r_hi_done")
        z2r_lo_done = sem("z2r_lo_done")
        zx_full, zx_hi, zx_lo = sem("zx_full"), sem("zx_hi"), sem("zx_lo")
        zc_full, zc_hi, zc_lo = sem("zc_full"), sem("zc_hi"), sem("zc_lo")
        yt_full, yt_hi, yt_lo = sem("yt_full"), sem("yt_hi"), sem("yt_lo")
        pt_full, pt_hi, pt_lo = sem("pt_full"), sem("pt_hi"), sem("pt_lo")
        t_full, t_hi, t_lo = sem("t_full"), sem("t_hi"), sem("t_lo")
        c_full, c_hi, c_lo = sem("c_full"), sem("c_hi"), sem("c_lo")
        r_full = sem("r_full")
        r_ready = sem("r_ready")
        s_full = sem("s_full")
        max_ready = sem("max_ready")
        top_ready = sem("top_ready")
        bias_ready = sem("bias_ready")
        exp_done = sem("exp_done")
        inv_ready = sem("inv_ready")
        probs_ready = sem("probs_ready")
        f_full = sem("f_full")
        res_ready = sem("res_ready")
        y_ready = sem("y_ready")
        y_bn_done = sem("y_bn_done")
        y_stats = sem("y_stats")
        y_ve_done = sem("y_ve_done")
        y_rstd_done = sem("y_rstd_done")
        yn_ready = sem("yn_ready")
        yf_ready = sem("yf_ready")
        h_full = sem("h_full")
        out_ready = sem("out_ready")

        def wait(eng, s, pair, per, n):
            v = pair * per + n
            if not isinstance(v, int) or v > 0:
                eng.wait_ge(s, v)

        def passes(hi_l, lo_l, hi_r, lo_r):
            return ((hi_l, hi_r), (hi_l, lo_r), (lo_l, hi_r))

        def steps(program):
            def run(eng):
                program(-1, False, True, True)
                program(0, True, True, True)
                with eng.Fori(1, PAIRS - 2) as i:
                    program(i, True, True, True)
                program(PAIRS - 2, True, True, False)
                program(PAIRS - 1, True, False, False)
            return run

        block = ctx.enter_context(nc.Block())

        @block.sync
        def _(sp):
            def load_x(p):
                for b in (0, 1):
                    sp.dma_start(x_in[:, b * T:(b + 1) * T, :].rearrange("p t d -> p (t d)"),
                                 x_rows[p, :, b, :]).then_inc(x_loaded, 16)

            def load_ctx(p, m):
                sp.dma_start(z2[:, m, :, :].rearrange("p (b t) d -> p b (t d)", b=2),
                             ctx_rows[m][p, :, :, :]).then_inc(ctx_loaded[m], 16)

            def load_res(p):
                for b in (0, 1):
                    sp.dma_start(x_res[:, b * T:(b + 1) * T, :].rearrange("p t d -> p (t d)"),
                                 x_rows[p, :, b, :]).then_inc(res_loaded, 16)

            def weight(dst, src, s):
                sp.dma_start(dst[:], src.rearrange("(c p) n -> p c n", p=P)).then_inc(s, 16)

            for key, (at, c) in vec_at.items():
                src = par(*key) if isinstance(key, tuple) else a["L0_xattn_" + key]
                sp.dma_start(vec_rows[at:at + c, :], src.rearrange("(c p) -> c p", p=P)).then_inc(s_vec, 16)
            weight(Wk[0], par(0, "Wk"), s_w["Wk0"])
            weight(Wq[0], par(0, "Wq"), s_w["Wq0"])
            load_x(0)
            weight(Wk[1], par(1, "Wk"), s_w["Wk1"])
            weight(Wq[1], par(1, "Wq"), s_w["Wq1"])
            for m in (0, 1):
                load_ctx(0, m)
            for m in (0, 1):
                weight(Wv[m], par(m, "Wv"), s_w[f"Wv{m}"])
                weight(Wo[m], par(m, "Wo"), s_w[f"Wo{m}"])
            weight(fcW, a["L0_xattn_fc_W"], s_w["fc"])
            for m in (0, 1):
                sp.dma_start(bo[:, m, :], par(m, "bo")[None, :].to_broadcast([P, D])).then_inc(s_w["rows"], 16)
            sp.dma_start(fcb[:], a["L0_xattn_fc_b"][None, :].to_broadcast([P, D])).then_inc(s_w["rows"], 16)
            load_res(0)
            wait(sp, z1_ready, 0, 4, 4)
            load_x(1)

            def body(i, back, front, norms):
                X, Y, Z = i, i + 1, i + 2
                if norms:
                    wait(sp, zc_full, Y, 4, 4)
                    wait(sp, z2r_lo_done, Y, 2, 2)
                    for m in (0, 1):
                        load_ctx(Z, m)
                    if not isinstance(i, int) or i + 3 < PAIRS:
                        wait(sp, z1_ready, Z, 4, 4)
                        load_x(i + 3)
                if back:
                    if front:
                        wait(sp, y_ready, X, 4, 4)
                        load_res(Y)
                    for b in (0, 1):
                        wait(sp, out_ready, X, 4, (b + 1) * T)
                        sp.dma_start(out_rows[X, :, b, :],
                                     y[:, b * T:(b + 1) * T, :].rearrange("p t d -> p (t d)")).then_inc(stored[b], 16)

            body(-1, False, True, True)
            body(0, True, True, True)
            with sp.Fori(1, PAIRS - 3) as i:
                body(i, True, True, True)
            body(PAIRS - 3, True, True, True)
            body(PAIRS - 2, True, True, False)
            body(PAIRS - 1, True, False, False)
            for b in (0, 1):
                sp.wait_ge(stored[b], 16 * PAIRS)

        @block.tensor
        def _(pe):
            def mm(out, l, r, start, stop):
                return nc.tensor.matmul(out, l, r, start=start, stop=stop)

            pe.wait_ge(s_vec, 16 * len(vec_at))
            pe.wait_ge(s_ident, 1)
            nc.tensor.transpose(turn[0][:, 0:NVEC], vec_rows[0:NVEC, :], ident[0:NVEC, 0:NVEC]).then_inc(s_vecT, 1)

            turned = [1]

            def turn_weight(src, rows, width_tiles):
                for e in range(EC):
                    k = turned[0]
                    if k == 4:
                        pe.wait_ge(s_vec_sb, 1)
                    if k > 4:
                        pe.wait_ge(s_ew, k - 4)
                    for r in range(rows):
                        last = nc.tensor.transpose(turn[k % 4][:, r * P:(r + 1) * P],
                                                   src[:, r, e * P:(e + 1) * P], ident[:])
                    last.then_inc(s_pw, 1)
                    turned[0] += 1

            def bias_cols(bank, at, w, chunks, m, name):
                for e in range(EC):
                    for c in range(chunks):
                        last = mm(bank[:, at + e:at + e + 1], w[:, c, e * P:(e + 1) * P], v_(m, name, c),
                                  c == 0, c == chunks - 1)
                return last

            pe.wait_ge(s_vec_sb, 1)
            for m in (0, 1):
                pe.wait_ge(s_w[f"Wk{m}"], 16)
                bias_cols(prod[m], 0, Wk[m], D2C, m, "ln2_b")
                pe.wait_ge(s_g, m + 1)
                turn_weight(Wkg[m], D2C, D2C)
                pe.wait_ge(s_w[f"Wq{m}"], 16)
                bias_cols(prod[m], 4, Wq[m], DC, m, "ln1_b").then_inc(s_bp, 1)
                turn_weight(Wq[m], DC, DC)
                pe.wait_ge(s_ew, 8 * m + 8)
                pe.wait_ge(s_bc, m + 1)
                pe.wait_ge(s_rep, 2 * m + 1)
                for j in range(D2C):
                    for e in range(EC):
                        mm(prod[m][:, 16 + j:17 + j], WkT[m][:, e, j * P:(j + 1) * P], col(BQ, m, e, e + 1),
                           e == 0, e == EC - 1)
                for j in range(DC):
                    for e in range(EC):
                        mm(prod[m][:, 20 + j:21 + j], WqT[m][:, e, j * P:(j + 1) * P], col(BK, m, e, e + 1),
                           e == 0, e == EC - 1)
                for e in range(EC):
                    last = mm(prod[m][:, 24:25], rep[:, 0, m, e, :], col(BK, m, e, e + 1), e == 0, e == EC - 1)
                last.then_inc(s_up, 1)
                for j in range(DC):
                    k = m * DC + j
                    if k >= 2:
                        pe.wait_ge(s_big_lo, k - 1)
                    for e in range(EC):
                        last = mm(prod[2 + k % 2][:, 0:D2], WqT[m][:, e, j * P:(j + 1) * P], WkT[m][:, e, :],
                                  e == 0, e == EC - 1)
                    last.then_inc(s_big, 1)
            for m in (0, 1):
                pe.wait_ge(s_w[f"Wv{m}"], 16)
                pe.wait_ge(s_uc, m + 1)
                bias_cols(prod[m], 0, Wv[m], D2C, m, "ln2_b").then_inc(s_bp, 1)
                turn_weight(Wv[m], D2C, D2C)
            for m in (0, 1):
                pe.wait_ge(s_ew, 16 + 4 * (m + 1))
                pe.wait_ge(s_w[f"Wo{m}"], 16)
                for j in range(D2C):
                    k = 2 * DC + m * D2C + j
                    pe.wait_ge(s_big_lo, k - 1)
                    for e in range(EC):
                        last = mm(prod[2 + k % 2][:], WvT[m][:, e, j * P:(j + 1) * P], Wo[m][:, e, :],
                                  e == 0, e == EC - 1)
                    last.then_inc(s_big, 1)
            pe.wait_ge(s_rep, 5)
            for m in (0, 1):
                for e in range(EC):
                    last = mm(prod[0][:], rep[:, 1, m, e, :], Wo[m][:, e, :], (m, e) == (0, 0), (m, e) == (1, EC - 1))
            last.then_inc(s_row, 1)
            pe.wait_ge(s_w["fc"], 16)
            for c in range(DC):
                last = mm(prod[1][:], ln_b_rep[:, c, :], fcW[:, c, :], c == 0, c == DC - 1)
            last.then_inc(s_row, 1)
            pe.wait_ge(s_ew, 24)
            pe.wait_ge(s_row_sb, 2)
            pe.wait_ge(s_big_lo, 2 * DC + 2 * D2C)

            def body(i, back, front, norms):
                X, Y = i, i + 1

                def turn_z1(k):
                    if k == 0:
                        wait(pe, z1_ready, Y, 4, 4)
                    wait(pe, pt_lo, X, 4, k + 1)
                    for n in range(TILES):
                        last = nc.tensor.transpose(turn[k][:, n * P:(n + 1) * P], z1[:, n, k * P:(k + 1) * P], ident[:])
                    last.then_inc(zx_full, 1)

                def context(k):
                    b, m = divmod(k, 2)
                    wait(pe, pt_lo, X, 4, k + 1)
                    wait(pe, out_ready, X - 1, 4, k + 1)
                    if b == 0:
                        wait(pe, z2r_lo_done, X, 2, m + 1)
                    for j in range(D2C):
                        for kt in range(T):
                            l = (z2r_hi[:, m, b * T + kt, j * P:(j + 1) * P], z2r_lo[:, m, b * T + kt, j * P:(j + 1) * P])
                            r = (share_hi[:, k, kt * S:(kt + 1) * S], share_lo[:, k, kt * S:(kt + 1) * S])
                            for q, (ll, rr) in enumerate(passes(*l, *r)):
                                last = mm(prod[k][:, j * S:(j + 1) * S], ll, rr, kt == 0 and q == 0,
                                          kt == T - 1 and q == 2)
                    last.then_inc(c_full, 1)

                def project(k):
                    m, j = divmod(k, D2C)
                    if back:
                        wait(pe, c_lo, X, 4, k + 1)
                    for c in range(DC):
                        if k == 0:
                            wait(pe, zx_lo, Y, 4, c + 1)
                        l = (M_hi[:, m, c, j * P:(j + 1) * P], M_lo[:, m, c, j * P:(j + 1) * P])
                        for q, (ll, rr) in enumerate(passes(*l, z1T_hi[:, c, :], z1T_lo[:, c, :])):
                            last = mm(prod[k][:], ll, rr, c == 0 and q == 0, c == DC - 1 and q == 2)
                    last.then_inc(t_full, 1)

                def turn_z2(k):
                    m, j = divmod(k, D2C)
                    wait(pe, z2_ready, Y, 8, 4 * m + 4)
                    wait(pe, zx_lo, Y, 4, k + 1)
                    for n in range(TILES):
                        last = nc.tensor.transpose(turn[k][:, n * P:(n + 1) * P], z2[:, m, n, j * P:(j + 1) * P], ident[:])
                    last.then_inc(zc_full, 1)

                def row_terms():
                    wait(pe, zc_lo, Y, 4, 4)
                    for n in range(TILES):
                        for c in range(DC):
                            l = (z1T_hi[:, c, n * P:(n + 1) * P], z1T_lo[:, c, n * P:(n + 1) * P])
                            for q, (ll, rr) in enumerate(passes(*l, w_hi[:, c, :], w_lo[:, c, :])):
                                last = mm(turn[3][:, 2 * n:2 * n + 2], ll, rr, c == 0 and q == 0, c == DC - 1 and q == 2)
                    last.then_inc(r_full, 1)

                def output(n):
                    b, t = divmod(n, T)
                    if t == 0:
                        wait(pe, c_lo, X, 4, 2 * b + 2)
                    if front:
                        wait(pe, t_lo, Y, 4, n + 1)
                    for m in (0, 1):
                        for j in range(D2C):
                            l = (cT_hi[:, b, m, j, t * P:(t + 1) * P], cT_lo[:, b, m, j, t * P:(t + 1) * P])
                            for q, (ll, rr) in enumerate(passes(*l, WA_hi[:, m, j, :], WA_lo[:, m, j, :])):
                                last = mm(prod[n][:], ll, rr, (m, j, q) == (0, 0, 0), (m, j, q) == (1, D2C - 1, 2))
                    last.then_inc(f_full, 1)

                def scores(k):
                    b, m = divmod(k, 2)
                    if k < 2:
                        wait(pe, t_lo, Y, 4, 2 * m + 2)
                        wait(pe, zc_lo, Y, 4, 2 * m + 2)
                    if back:
                        wait(pe, y_ready, X, 4, k + 1)
                    for t in range(T):
                        n = b * T + t
                        for j in range(D2C):
                            l = (tT_hi[:, m, j, n * P:(n + 1) * P], tT_lo[:, m, j, n * P:(n + 1) * P])
                            r = (z2T_hi[:, m, j, b * S:(b + 1) * S], z2T_lo[:, m, j, b * S:(b + 1) * S])
                            for q, (ll, rr) in enumerate(passes(*l, *r)):
                                last = mm(prod[k][:, t * S:(t + 1) * S], ll, rr, j == 0 and q == 0,
                                          j == D2C - 1 and q == 2)
                    last.then_inc(s_full, 1)

                def turn_y(n):
                    wait(pe, yn_ready, X, 4, n + 1)
                    if front:
                        wait(pe, zc_lo, Y, 4, n + 1)
                        if n == 3:
                            wait(pe, r_ready, Y, 1, 1)
                    for c in range(DC):
                        last = nc.tensor.transpose(turn[n][:, c * P:(c + 1) * P], yn[:, n, c * P:(c + 1) * P], ident[:])
                    last.then_inc(yt_full, 1)

                def linear(n):
                    wait(pe, yt_lo, X, 4, n + 1)
                    if front:
                        wait(pe, exp_done, Y, 8, 2 * n + 2)
                    for c in range(DC):
                        l = (share_hi[:, n, c * P:(c + 1) * P], share_lo[:, n, c * P:(c + 1) * P])
                        for q, (ll, rr) in enumerate(passes(*l, fc_hi[:, c, :], fc_lo[:, c, :])):
                            last = mm(prod[n][:], ll, rr, c == 0 and q == 0, c == DC - 1 and q == 2)
                    last.then_inc(h_full, 1)

                def turn_probs(k):
                    b, m = divmod(k, 2)
                    wait(pe, probs_ready, Y, 8, 2 * k + 2)
                    if back:
                        wait(pe, yt_lo, X, 4, k + 1)
                    elif k == 3:
                        wait(pe, r_ready, Y, 1, 1)
                    for kt in range(T):
                        for t in range(T):
                            last = nc.tensor.transpose(turn[k][:, kt * S + t * P:kt * S + (t + 1) * P],
                                                       probs[:, b, m, t, kt * P:(kt + 1) * P], ident[:])
                    last.then_inc(pt_full, 1)

                for k in range(4):
                    if front:
                        turn_z1(k)
                    if back:
                        context(k)
                if front:
                    for k in range(4):
                        project(k)
                        turn_z2(k)
                for n in range(4):
                    if back:
                        output(n)
                    if front and n == 0:
                        row_terms()
                for k in range(4):
                    if front:
                        scores(k)
                    if back:
                        turn_y(k)
                for n in range(4):
                    if back:
                        linear(n)
                    if front and n > 0:
                        turn_probs(n - 1)
                if front:
                    turn_probs(3)

            steps(body)(pe)

        @block.scalar
        def _(act):
            def hi(out, in_, **kw):
                return nc.scalar.activation(out, in_, ACT.Identity if "bias" in kw else ACT.Copy, **kw)

            evac = 0
            act.wait_ge(s_vec_sb, 1)
            for m in (0, 1):
                for name, dst, rows in (("Wk", WkT[m], D2C), ("Wq", WqT[m], DC)):
                    for e in range(EC):
                        act.wait_ge(s_pw, evac + 1)
                        act.wait_ge(s_ew, evac)
                        nc.scalar.copy(dst[:, e, :], turn[(evac + 1) % 4][:, 0:rows * P]).then_inc(s_ew, 1)
                        evac += 1
                act.wait_ge(s_uc, m + 1)
                for j in range(DC):
                    act.wait_ge(s_big, m * DC + j + 1)
                    k = m * DC + j
                    hi(M_hi[:, m, j, :], prod[2 + k % 2][:, 0:D2], scale=col(G1S, m, j, j + 1)).then_inc(s_big_hi, 1)
            for m in (0, 1):
                for e in range(EC):
                    act.wait_ge(s_pw, evac + 1)
                    nc.scalar.copy(WvT[m][:, e, :], turn[(evac + 1) % 4][:, 0:D2]).then_inc(s_ew, 1)
                    evac += 1
            for m in (0, 1):
                for j in range(D2C):
                    k = 2 * DC + m * D2C + j
                    act.wait_ge(s_big, k + 1)
                    hi(WA_hi[:, m, j, :], prod[2 + k % 2][:], scale=v_(m, "ln2_g", j)).then_inc(s_big_hi, 1)
            act.wait_ge(s_w["fc"], 16)
            for c in range(DC):
                g = vec_at["ln_g"][0] + c
                hi(fc_hi[:, c, :], fcW[:, c, :], scale=vec[:, g:g + 1]).then_inc(s_fc_hi, 1)

            def body(i, back, front, norms):
                X, Y = i, i + 1
                for k in range(4):
                    if front:
                        wait(act, zx_full, Y, 4, k + 1)
                        hi(z1T_hi[:, k, :], turn[k][:]).then_inc(zx_hi, 1)
                    if back:
                        b, m = divmod(k, 2)
                        wait(act, c_full, X, 4, k + 1)
                        hi(cT_hi[:, b, m, :, :].rearrange("p j s -> p (j s)"), prod[k][:]).then_inc(c_hi, 1)
                if front:
                    for k in range(4):
                        m, j = divmod(k, D2C)
                        if j == 0:
                            wait(act, z2_ready, Y, 8, 4 * m + 4)
                            hi(z2r_hi[:, m, :, :].rearrange("p n d -> p (n d)"),
                               z2[:, m, :, :].rearrange("p n d -> p (n d)")).then_inc(z2r_hi_done, 1)
                        wait(act, t_full, Y, 4, k + 1)
                        hi(tT_hi[:, m, j, :], prod[k][:], bias=u_col[:, m, j:j + 1]).then_inc(t_hi, 1)
                        wait(act, zc_full, Y, 4, k + 1)
                        hi(z2T_hi[:, m, j, :], turn[k][:]).then_inc(zc_hi, 1)
                for k in range(4):
                    if front:
                        b, m = divmod(k, 2)
                        wait(act, bias_ready, Y, 4, k + 1)
                        for t in range(T):
                            nc.scalar.activation(probs[:, b, m, t, :], prod[k][:, t * S:(t + 1) * S], ACT.Exp,
                                                 bias=exp_bias[:, b, m, t:t + 1],
                                                 accum_out=exp_sum[:, b, m, t:t + 1]).then_inc(exp_done, 1)
                    if back:
                        wait(act, yt_full, X, 4, k + 1)
                        hi(share_hi[:, k, :], turn[k][:]).then_inc(yt_hi, 1)
                if front:
                    for k in range(4):
                        wait(act, pt_full, Y, 4, k + 1)
                        hi(share_hi[:, k, :], turn[k][:]).then_inc(pt_hi, 1)

            steps(body)(act)

        @block.vector
        def _(dve):
            def lo(out, in_, h):
                return nc.vector.tensor_tensor(out, in_, h.bitcast(F32), ALU.subtract)

            def lo_scaled(out, in_, s, h):
                return nc.vector.scalar_tensor_tensor(out, in_, s, h.bitcast(F32), ALU.mult, ALU.subtract)

            def x_bn_stats(p):
                wait(dve, x_loaded, p, 32, 32)
                for n in range(TILES):
                    nc.vector.bn_stats(x_bn[:, n, :], x_in[:, n, :]).then_inc(x_bn_done, 1)

            def x_bn_wait(p):
                wait(dve, x_bn_done, p, 4, 4)

            def x_bn_aggr():
                for n in range(TILES):
                    nc.vector.bn_aggr(x_mv[:, n, :], x_bn[:, n, :]).then_inc(x_stats, 1)

            def norm_x(p, n):
                wait(dve, x_rstd_done, p, 1, 1)
                nc.vector.tensor_scalar(z1[:, n, :], x_in[:, n, :], x_mv[:, n, 0:1], x_rstd[:, n:n + 1],
                                        ALU.subtract, ALU.mult).then_inc(z1_ready, 1)

            def ctx_bn_stats(p, m):
                wait(dve, ctx_loaded[m], p, 16, 16)
                for n in range(TILES):
                    nc.vector.bn_stats(ctx_bn[:, m, n, :], z2[:, m, n, :]).then_inc(ctx_bn_done, 1)

            def ctx_bn_wait(p, m):
                wait(dve, ctx_bn_done, p, 8, 4 * m + 4)

            def ctx_bn_aggr(m):
                for n in range(TILES):
                    nc.vector.bn_aggr(ctx_mv[:, m, n, :], ctx_bn[:, m, n, :]).then_inc(ctx_stats, 1)

            def norm_ctx(p, m):
                wait(dve, ctx_rstd_done, p, 2, m + 1)
                for n in range(TILES):
                    nc.vector.tensor_scalar(z2[:, m, n, :], z2[:, m, n, :], ctx_mv[:, m, n, 0:1],
                                            ctx_rstd[:, m, n:n + 1], ALU.subtract, ALU.mult).then_inc(z2_ready, 1)

            nc.vector.memset(ones[:], 1.0).then_inc(s_const, 1)
            dve.wait_ge(s_vecT, 1)
            nc.vector.tensor_copy(vec[:, 0:NVEC], turn[0][:, 0:NVEC]).then_inc(s_vec_sb, 1)
            dve.wait_ge(s_vec_sb, 1)
            dve.wait_ge(s_const, 1)
            big = 0
            for m in (0, 1):
                dve.wait_ge(s_w[f"Wk{m}"], 16)
                for c in range(D2C):
                    g = nc.vector.tensor_scalar(Wkg[m][:, c, :], Wk[m][:, c, :], v_(m, "ln2_g", c), None, ALU.mult)
                g.then_inc(s_g, 1)
                at = vec_at[m, "ln1_g"][0]
                nc.vector.tensor_scalar(col(G1S, m, 0, 4), vec[:, at:at + 4], SCALE, None, ALU.mult)
                dve.wait_ge(s_bp, m + 1)
                at = vec_at[m, "bk"][0]
                nc.vector.tensor_tensor(col(BK, m, 0, 4), prod[m][:, 0:4], vec[:, at:at + 4], ALU.add)
                at = vec_at[m, "bq"][0]
                nc.vector.tensor_tensor(col(BQ, m, 0, 4), prod[m][:, 4:8], vec[:, at:at + 4], ALU.add).then_inc(s_bc, 1)
                dve.wait_ge(s_bc, m + 1)
                for e in range(EC):
                    last = nc.vector.tensor_scalar(rep[:, 0, m, e, :], ones[:], col(BQ, m, e, e + 1), None, ALU.mult)
                last.then_inc(s_rep, 1)
                if m == 0:
                    x_bn_stats(0)
                    x_bn_wait(0)
                    x_bn_aggr()
                    for n in range(TILES):
                        norm_x(0, n)
                    at = vec_at["ln_b"][0]
                    for e in range(DC):
                        last = nc.vector.tensor_scalar(ln_b_rep[:, e, :], ones[:], vec[:, at + e:at + e + 1], None, ALU.mult)
                    last.then_inc(s_rep, 1)
                dve.wait_ge(s_up, m + 1)
                nc.vector.tensor_scalar(u_col[:, m, :], prod[m][:, 16:18], SCALE, None, ALU.mult)
                for n in range(TILES):
                    nc.vector.tensor_scalar(r0[:, n, m:m + 1], prod[m][:, 24:25], SCALE, None, ALU.mult)
                w_tmp = cols[:, 40 + 4 * m:44 + 4 * m]
                nc.vector.tensor_tensor(w_tmp, prod[m][:, 20:24], col(G1S, m, 0, 4), ALU.mult).then_inc(s_uc, 1)
                dve.wait_ge(s_uc, m + 1)
                nc.vector.tensor_copy(w_hi[:, :, m], w_tmp).then_inc(s_wc, 1)
                dve.wait_ge(s_wc, m + 1)
                nc.vector.tensor_tensor(w_lo[:, :, m], w_tmp, w_hi[:, :, m].bitcast(F32), ALU.subtract).then_inc(s_r0, 1)
                for j in range(DC):
                    k = m * DC + j
                    dve.wait_ge(s_big_hi, k + 1)
                    lo_scaled(M_lo[:, m, j, :], prod[2 + k % 2][:, 0:D2], col(G1S, m, j, j + 1),
                              M_hi[:, m, j, :]).then_inc(s_big_lo, 1)
            for m in (0, 1):
                ctx_bn_stats(0, m)
                ctx_bn_wait(0, m)
                ctx_bn_aggr(m)
            for m in (0, 1):
                norm_ctx(0, m)
            for m in (0, 1):
                dve.wait_ge(s_bp, 3 + m)
                at = vec_at[m, "bv"][0]
                nc.vector.tensor_tensor(col(BV, m, 0, 4), prod[m][:, 0:4], vec[:, at:at + 4], ALU.add).then_inc(s_bc, 1)
                dve.wait_ge(s_bc, 3 + m)
                for e in range(EC):
                    last = nc.vector.tensor_scalar(rep[:, 1, m, e, :], ones[:], col(BV, m, e, e + 1), None, ALU.mult)
                last.then_inc(s_rep, 1)
            for m in (0, 1):
                for j in range(D2C):
                    k = 2 * DC + m * D2C + j
                    dve.wait_ge(s_big_hi, k + 1)
                    lo_scaled(WA_lo[:, m, j, :], prod[2 + k % 2][:], v_(m, "ln2_g", j), WA_hi[:, m, j, :]).then_inc(s_big_lo, 1)
            dve.wait_ge(s_w["rows"], 48)
            nc.vector.tensor_tensor(bo[:, 0, :], bo[:, 0, :], bo[:, 1, :], ALU.add).then_inc(s_bo, 1)
            for c in range(DC):
                g = vec_at["ln_g"][0] + c
                dve.wait_ge(s_fc_hi, c + 1)
                lo_scaled(fc_lo[:, c, :], fcW[:, c, :], vec[:, g:g + 1], fc_hi[:, c, :]).then_inc(s_fc_lo, 1)
            dve.wait_ge(s_bo, 1)
            dve.wait_ge(s_row, 1)
            nc.vector.tensor_tensor(c_row[:], prod[0][:], bo[:, 0, :], ALU.add).then_inc(s_row_sb, 1)
            dve.wait_ge(s_row, 2)
            nc.vector.tensor_tensor(f_row[:], prod[1][:], fcb[:], ALU.add).then_inc(s_row_sb, 1)

            def body(i, back, front, norms):
                X, Y, Z = i, i + 1, i + 2
                for k in range(4):
                    if front:
                        wait(dve, zx_hi, Y, 4, k + 1)
                        lo(z1T_lo[:, k, :], turn[k][:], z1T_hi[:, k, :]).then_inc(zx_lo, 1)
                    if back:
                        b, m = divmod(k, 2)
                        wait(dve, c_hi, X, 4, k + 1)
                        lo(cT_lo[:, b, m, :, :].rearrange("p j s -> p (j s)"), prod[k][:],
                           cT_hi[:, b, m, :, :].rearrange("p j s -> p (j s)")).then_inc(c_lo, 1)
                if norms:
                    x_bn_stats(Z)
                if front:
                    for k in range(4):
                        m, j = divmod(k, D2C)
                        wait(dve, t_hi, Y, 4, k + 1)
                        if norms and k == 0:
                            x_bn_wait(Z)
                        nc.vector.scalar_tensor_tensor(tT_lo[:, m, j, :], prod[k][:], u_col[:, m, j:j + 1],
                                                       tT_hi[:, m, j, :].bitcast(F32), ALU.add,
                                                       ALU.subtract).then_inc(t_lo, 1)
                        if norms and k == 0:
                            x_bn_aggr()
                        wait(dve, zc_hi, Y, 4, k + 1)
                        lo(z2T_lo[:, m, j, :], turn[k][:], z2T_hi[:, m, j, :]).then_inc(zc_lo, 1)
                if norms:
                    for n in range(TILES):
                        norm_x(Z, n)
                def norm_y(n):
                    wait(dve, y_rstd_done, X, 4, n + 1)
                    nc.vector.tensor_scalar(yn[:, n, :], y[:, n, :], y_mv[:, n, 0:1], y_rstd[:, n:n + 1],
                                            ALU.subtract, ALU.mult).then_inc(yn_ready, 1)

                for n in range(4):
                    if back:
                        wait(dve, f_full, X, 4, n + 1)
                        wait(dve, res_ready, X, 4, n + 1)
                        wait(dve, stored[n // T], X - 1, 16, 16)
                        nc.vector.tensor_tensor(y[:, n, :], prod[n][:], x_res[:, n, :], ALU.add).then_inc(y_ready, 1)
                        wait(dve, y_ready, X, 4, n + 1)
                        nc.vector.bn_stats(y_bn[:, n, :], y[:, n, :]).then_inc(y_bn_done, 1)
                        wait(dve, y_bn_done, X, 4, n + 1)
                    if front and n == 0:
                        wait(dve, r_full, Y, 1, 1)
                        nc.vector.tensor_tensor(r_sb[:].rearrange("p n m -> p (n m)"), turn[3][:, 0:2 * TILES],
                                                r0[:].rearrange("p n m -> p (n m)"), ALU.add).then_inc(r_ready, 1)
                    if back:
                        if n > 0:
                            norm_y(n - 1)
                        nc.vector.bn_aggr(y_mv[:, n, :], y_bn[:, n, :]).then_inc(y_stats, 1)
                for k in range(4):
                    b, m = divmod(k, 2)
                    if front:
                        wait(dve, s_full, Y, 4, k + 1)
                        nc.vector.tensor_reduce(neg_max[:, b, m, :], prod[k][:].rearrange("p (t s) -> p t s", t=T),
                                                AX_X, ALU.max, negate=True).then_inc(max_ready, 1)
                    if back:
                        if k == 0:
                            norm_y(3)
                        wait(dve, yt_hi, X, 4, k + 1)
                        lo(share_lo[:, k, :], turn[k][:], share_hi[:, k, :]).then_inc(yt_lo, 1)

                def normalise(k):
                    b, m = divmod(k, 2)
                    wait(dve, exp_done, Y, 8, 2 * k + 2)
                    nc.vector.reciprocal(exp_inv[:, b, m, :], exp_sum[:, b, m, :]).then_inc(inv_ready, 1)
                    wait(dve, inv_ready, Y, 4, k + 1)
                    for t in range(T):
                        nc.vector.tensor_scalar(probs[:, b, m, t, :], probs[:, b, m, t, :], exp_inv[:, b, m, t:t + 1],
                                                None, ALU.mult).then_inc(probs_ready, 1)

                if front:
                    for k in range(4):
                        normalise(k)
                for n in range(4):
                    if norms and n < 2:
                        ctx_bn_stats(Z, n)
                        ctx_bn_wait(Z, n)
                    if back:
                        wait(dve, h_full, X, 4, n + 1)
                        wait(dve, yf_ready, X, 4, n + 1)
                        nc.vector.tensor_tensor(y[:, n, :], prod[n][:], y[:, n, :], ALU.add).then_inc(out_ready, 1)
                    if norms:
                        if n < 2:
                            ctx_bn_aggr(n)
                        else:
                            norm_ctx(Z, n - 2)
                    if front and n > 0:
                        wait(dve, pt_hi, Y, 4, n)
                        lo(share_lo[:, n - 1, :], turn[n - 1][:], share_hi[:, n - 1, :]).then_inc(pt_lo, 1)
                if front:
                    wait(dve, pt_hi, Y, 4, 4)
                    lo(share_lo[:, 3, :], turn[3][:], share_hi[:, 3, :]).then_inc(pt_lo, 1)

            steps(body)(dve)

        @block.gpsimd
        def _(pool):
            nc.gpsimd.memset(ident[:], 0.0).then_inc(s_ident0, 1)
            pool.wait_ge(s_ident0, 1)
            nc.gpsimd.affine_select(out=ident[:], in_=ident[:], compare_op=ALU.not_equal, fill=1.0, base=0,
                                    pattern=[[-1, P]], channel_multiplier=1).then_inc(s_ident, 1)
            nc.gpsimd.memset(minus_half[:], -0.5).then_inc(s_ident0, 1)
            nc.gpsimd.memset(eps[:], EPS).then_inc(s_ident0, 1)
            pool.wait_ge(s_ident0, 3)

            def rstd(ve, out, mv, width, stats, stats_at, ve_done, ve_at, done):
                wait(pool, stats, *stats_at)
                nc.gpsimd.tensor_tensor(ve, mv, eps[:, 0:width], ALU.add).then_inc(ve_done, 1)
                wait(pool, ve_done, *ve_at)
                nc.gpsimd.tensor_tensor(out, ve, minus_half[:, 0:width], ALU.pow).then_inc(done, 1)

            def rstd_x(p):
                rstd(x_ve[:], x_rstd[:], x_mv[:, :, 1], TILES, x_stats, (p, 4, 4), x_ve_done, (p, 1, 1), x_rstd_done)

            def rstd_ctx(p, m):
                rstd(ctx_ve[:, m, :], ctx_rstd[:, m, :], ctx_mv[:, m, :, 1], TILES, ctx_stats, (p, 8, 4 * m + 4),
                     ctx_ve_done, (p, 2, m + 1), ctx_rstd_done)

            rstd_x(0)
            rstd_ctx(0, 0)
            rstd_ctx(0, 1)

            def body(i, back, front, norms):
                X, Y, Z = i, i + 1, i + 2
                if back:
                    wait(pool, res_loaded, X, 32, 32)
                    if isinstance(i, int) and i == 0:
                        pool.wait_ge(s_row_sb, 2)
                    for n in range(TILES):
                        nc.gpsimd.tensor_tensor(x_res[:, n, :], x_res[:, n, :], c_row[:], ALU.add).then_inc(res_ready, 1)
                if norms:
                    rstd_x(Z)
                if front:
                    for m in (0, 1):
                        wait(pool, z2r_hi_done, Y, 2, m + 1)
                        nc.gpsimd.tensor_tensor(z2r_lo[:, m, :, :].rearrange("p n d -> p (n d)"),
                                                z2[:, m, :, :].rearrange("p n d -> p (n d)"),
                                                z2r_hi[:, m, :, :].rearrange("p n d -> p (n d)").bitcast(F32),
                                                ALU.subtract).then_inc(z2r_lo_done, 1)
                if back:
                    for n in range(TILES):
                        rstd(y_ve[:, n:n + 1], y_rstd[:, n:n + 1], y_mv[:, n, 1:2], 1, y_stats, (X, 4, n + 1),
                             y_ve_done, (X, 4, n + 1), y_rstd_done)
                if front:
                    for k in range(4):
                        b, m = divmod(k, 2)
                        if k == 0:
                            wait(pool, r_ready, Y, 1, 1)
                        wait(pool, max_ready, Y, 4, k + 1)
                        r = r_sb[:, b * T:(b + 1) * T, m]
                        nc.gpsimd.tensor_tensor(neg_top[:, b, m, :], neg_max[:, b, m, :], r, ALU.subtract).then_inc(top_ready, 1)
                        wait(pool, top_ready, Y, 4, k + 1)
                        nc.gpsimd.tensor_tensor(exp_bias[:, b, m, :], neg_top[:, b, m, :], r, ALU.add).then_inc(bias_ready, 1)
                if back:
                    for n in range(TILES):
                        wait(pool, yn_ready, X, 4, n + 1)
                        nc.gpsimd.tensor_tensor(y[:, n, :], y[:, n, :], f_row[:], ALU.add).then_inc(yf_ready, 1)
                if norms:
                    for m in (0, 1):
                        rstd_ctx(Z, m)

            steps(body)(pool)


def kernel(**inputs):
    import numpy as _np
    import concourse.bacc as _bacc
    from concourse import mybir as _mybir
    from concourse.bass_utils import run_bass_kernel_spmd as _run

    nc = _bacc.Bacc("TRN2", target_bir_lowering=False, num_devices=1)
    arrays, aps = {}, {}
    for name, value in inputs.items():
        v = _np.ascontiguousarray(value)
        arrays[f"in_{name}_dram"] = v
        aps[name] = nc.dram_tensor(f"in_{name}_dram", v.shape, _mybir.dt.from_np(v.dtype), kind="ExternalInput").ap()
    aps["out"] = nc.dram_tensor("out_0_dram", inputs["x"].shape, _mybir.dt.float32, kind="ExternalOutput").ap()
    build(nc, aps)
    r = _run(nc, [arrays], core_ids=[0])
    return r.results[0]["out_0_dram"]
```

```python
from contextlib import ExitStack

import concourse.bass as bass
from concourse import mybir

F32 = mybir.dt.float32
F32R = mybir.dt.float32r
ALU = mybir.AluOpType
ACT = mybir.ActivationFunctionType
AX_X = mybir.AxisListType.X
P = 128
EPS = 1e-5


def build(nc, a):
    B, S, D = a["x"].shape
    D2 = a["ctx_512"].shape[2]
    E = a["L0_xattn_a_Wq"].shape[1]
    MODS = ("a", "v")
    DC, EC, D2C = D // P, E // P, D2 // P
    T = S // P
    TILES = 2 * T
    PAIRS = B // 2
    ROWS = TILES * P
    SCALE = float(E) ** -0.5
    assert T == 2 and D2C == 2 and DC == 4 and EC == 4 and D == 512 and S == 256

    x_rows = a["x"].rearrange("(i b) (p t) d -> i p b (t d)", b=2, t=T)
    out_rows = a["out"].rearrange("(i b) (p t) d -> i p b (t d)", b=2, t=T)
    ctx_rows = [a[n].rearrange("(i b) (p t) d -> i p b (t d)", b=2, t=T)
                for n in ("ctx_512", "fside_BxSxS_0")]

    def par(m, name):
        return a[f"L0_xattn_{MODS[m]}_{name}"]

    ctx = ExitStack()
    with ctx:
        def sb(name, shape, dt=F32, stack=ctx):
            return stack.enter_context(nc.sbuf_tensor(name, shape, dt))

        def sem(name):
            return ctx.enter_context(nc.semaphore(name))

        prod = [ctx.enter_context(nc.psum_tensor(f"prod{k}", [P, 512], F32)) for k in range(4)]
        turn = [ctx.enter_context(nc.psum_tensor(f"turn{k}", [P, 512], F32)) for k in range(4)]

        M_hi = sb("M_hi", [P, 2, DC, D2], F32R)
        M_lo = sb("M_lo", [P, 2, DC, D2], F32R)
        WA_hi = sb("WA_hi", [P, 2, D2C, D], F32R)
        WA_lo = sb("WA_lo", [P, 2, D2C, D], F32R)
        fc_hi = sb("fc_hi", [P, DC, D], F32R)
        fc_lo = sb("fc_lo", [P, DC, D], F32R)
        c_row = sb("c_row", [P, D])
        f_row = sb("f_row", [P, D])
        ident = sb("ident", [P, P])
        u_col = sb("u_col", [P, 2, D2C])
        w_row = sb("w_row", [P, 2, D])
        r0 = sb("r0", [P, TILES, 2])
        minus_half = sb("minus_half", [P, TILES])
        eps = sb("eps", [P, TILES])

        x_bn = sb("x_bn", [P, TILES, 6])
        x_mv = sb("x_mv", [P, TILES, 2])
        x_ve = sb("x_ve", [P, TILES])
        x_rstd = sb("x_rstd", [P, TILES])
        ctx_bn = sb("ctx_bn", [P, 2, TILES, 6])
        ctx_mv = sb("ctx_mv", [P, 2, TILES, 2])
        ctx_ve = sb("ctx_ve", [P, 2, TILES])
        ctx_rstd = sb("ctx_rstd", [P, 2, TILES])
        y_bn = sb("y_bn", [P, TILES, 6])
        y_mv = sb("y_mv", [P, TILES, 2])
        y_ve = sb("y_ve", [P, TILES])
        y_rstd = sb("y_rstd", [P, TILES])
        r_sum = sb("r_sum", [P, TILES, 2])
        r_sb = sb("r_sb", [P, TILES, 2])
        neg_max = sb("neg_max", [P, 2, 2, T])
        neg_top = sb("neg_top", [P, 2, 2, T])
        exp_bias = sb("exp_bias", [P, 2, 2, T])
        exp_sum = sb("exp_sum", [P, 2, 2, T])
        exp_inv = sb("exp_inv", [P, 2, 2, T])

        x_in = sb("x_in", [P, TILES, D])
        x_res = sb("x_res", [P, TILES, D])
        z1 = sb("z1", [P, TILES, D])
        z2 = sb("z2", [P, 2, TILES, D2])
        probs = sb("probs", [P, 2, 2, T, S])
        y = sb("y", [P, TILES, D])
        yn = sb("yn", [P, 2, D])

        early = ExitStack()
        Wq = [sb(f"Wq{m}", [P, DC, E], stack=early) for m in (0, 1)]
        WqT = [sb(f"WqT{m}", [P, EC, D], stack=early) for m in (0, 1)]
        Wk = [sb(f"Wk{m}", [P, D2C, E], stack=early) for m in (0, 1)]
        WkT = [sb(f"WkT{m}", [P, EC, D2], stack=early) for m in (0, 1)]
        Wv = [sb(f"Wv{m}", [P, D2C, E], stack=early) for m in (0, 1)]
        WvT = [sb(f"WvT{m}", [P, EC, D2], stack=early) for m in (0, 1)]
        Wo = [sb(f"Wo{m}", [P, EC, D], stack=early) for m in (0, 1)]
        Wkg = [probs[:, m, :, :, :].rearrange("p m t s -> p (m t s)").rearrange("p (c e) -> p c e", c=D2C) for m in (0, 1)]
        fcW = y
        bo = sb("bo", [P, 2, D], stack=early)
        fcb = sb("fcb", [P, D], stack=early)
        bq_row = sb("bq_row", [P, 2, E], stack=early)
        bk_row = sb("bk_row", [P, 2, E], stack=early)
        scratch = sb("scratch", [P, E], stack=early)
        ones = sb("ones", [P, P], stack=early)
        b1_rep = x_res[:, 0:2, :].rearrange("p n d -> p (n d)").rearrange("p (m c q) -> p m c q", m=2, c=DC)
        bv_rep = x_res[:, 2:4, :].rearrange("p n d -> p (n d)").rearrange("p (m c q) -> p m c q", m=2, c=EC)
        b2_rep = yn[:, 0, :].rearrange("p (m c q) -> p m c q", m=2, c=D2C)
        ln_b_rep = yn[:, 1, :].rearrange("p (c q) -> p c q", c=DC)
        vec_rows = sb("vec_rows", [64, P], stack=early)
        vec = sb("vec", [P, 64], stack=early)
        cols = sb("cols", [P, 64], stack=early)
        early.close()

        z2r_hi = sb("z2r_hi", [P, 2, TILES, D2], F32R)
        z2r_lo = sb("z2r_lo", [P, 2, TILES, D2], F32R)
        z1T_hi = sb("z1T_hi", [P, DC, ROWS], F32R)
        z1T_lo = sb("z1T_lo", [P, DC, ROWS], F32R)
        z2T_hi = sb("z2T_hi", [P, 2, D2C, ROWS], F32R)
        z2T_lo = sb("z2T_lo", [P, 2, D2C, ROWS], F32R)
        tT_hi = sb("tT_hi", [P, 2, D2C, ROWS], F32R)
        tT_lo = sb("tT_lo", [P, 2, D2C, ROWS], F32R)
        cT_hi = sb("cT_hi", [P, 2, 2, D2C, S], F32R)
        cT_lo = sb("cT_lo", [P, 2, 2, D2C, S], F32R)
        share_hi = sb("share_hi", [P, 4, 512], F32R)
        share_lo = sb("share_lo", [P, 4, 512], F32R)

        vec_at, n = {}, 0
        for m in (0, 1):
            for name, c in (("ln1_g", DC), ("ln1_b", DC), ("ln2_g", D2C), ("ln2_b", D2C),
                            ("bq", EC), ("bk", EC), ("bv", EC)):
                vec_at[m, name] = (n, c)
                n += c
        for name in ("ln_g", "ln_b"):
            vec_at[name] = (n, DC)
            n += DC
        NVEC = n

        def v_(m, name, k):
            at = vec_at[m, name][0] + k
            return vec[:, at:at + 1]

        def col(kind, m, k0, k1):
            at = (kind * 2 + m) * 4
            return cols[:, at + k0:at + k1]

        G1S, WB, W, BV = range(4)

        vec_loaded = sem("vec_loaded")
        ld = {k: sem(k + "_loaded") for k in ("Wq0", "Wq1", "Wk0", "Wk1", "Wv0", "Wv1", "Wo0", "Wo1", "fcW",
                                              "b0", "b1", "rows")}
        zeroed = sem("zeroed")
        ident_ready = sem("ident_ready")
        ones_ready = sem("ones_ready")
        vec_turned = sem("vec_turned")
        vec_ready = sem("vec_ready")
        wkg_ready = sem("wkg_ready")
        g1s_ready = sem("g1s_ready")
        b_rep_ready = sem("b_rep_ready")
        ln_rep_ready = sem("ln_rep_ready")
        w_turned = sem("w_turned")
        w_copied = sem("w_copied")
        qk_rows = sem("qk_rows")
        qk_rows_sb = sem("qk_rows_sb")
        dots = sem("dots")
        w_col_ready = sem("w_col_ready")
        diag_ready = sem("diag_ready")
        w_row_full = sem("w_row_full")
        w_row_ready = sem("w_row_ready")
        bv_cols = sem("bv_cols")
        bv_ready = sem("bv_ready")
        bv_rep_ready = sem("bv_rep_ready")
        big_full = sem("big_full")
        big_hi = sem("big_hi")
        big_lo = sem("big_lo")
        rows_full = sem("rows_full")
        rows_ready = sem("rows_ready")
        bo_summed = sem("bo_summed")
        fc_hi_done = sem("fc_hi_done")
        fc_lo_done = sem("fc_lo_done")

        x_loaded = sem("x_loaded")
        ctx_loaded = [sem("ctxa_loaded"), sem("ctxv_loaded")]
        res_loaded = sem("res_loaded")
        stored = [sem("stored0"), sem("stored1")]
        x_bn_done = sem("x_bn_done")
        x_stats = sem("x_stats")
        x_ve_done = sem("x_ve_done")
        x_rstd_done = sem("x_rstd_done")
        z1_ready = sem("z1_ready")
        ctx_bn_done = sem("ctx_bn_done")
        ctx_stats = sem("ctx_stats")
        ctx_ve_done = sem("ctx_ve_done")
        ctx_rstd_done = sem("ctx_rstd_done")
        z2_ready = sem("z2_ready")
        z2r_hi_done = sem("z2r_hi_done")
        z2r_lo_done = sem("z2r_lo_done")
        zx_full, zx_hi, zx_lo = sem("zx_full"), sem("zx_hi"), sem("zx_lo")
        zc_full, zc_hi, zc_lo = sem("zc_full"), sem("zc_hi"), sem("zc_lo")
        yt_full, yt_hi, yt_lo = sem("yt_full"), sem("yt_hi"), sem("yt_lo")
        pt_full, pt_hi, pt_lo = sem("pt_full"), sem("pt_hi"), sem("pt_lo")
        t_full, t_hi, t_lo = sem("t_full"), sem("t_hi"), sem("t_lo")
        c_full, c_hi, c_lo = sem("c_full"), sem("c_hi"), sem("c_lo")
        r_product = sem("r_product")
        r_summed = sem("r_summed")
        r_ready = sem("r_ready")
        s_full = sem("s_full")
        max_ready = sem("max_ready")
        top_ready = sem("top_ready")
        bias_ready = sem("bias_ready")
        exp_done = sem("exp_done")
        inv_ready = sem("inv_ready")
        probs_ready = sem("probs_ready")
        f_full = sem("f_full")
        res_ready = sem("res_ready")
        y_ready = sem("y_ready")
        y_bn_done = sem("y_bn_done")
        y_stats = sem("y_stats")
        y_ve_done = sem("y_ve_done")
        y_rstd_done = sem("y_rstd_done")
        yn_ready = sem("yn_ready")
        yf_ready = sem("yf_ready")
        h_full = sem("h_full")
        out_ready = sem("out_ready")

        def wait(eng, s, pair, per, n):
            v = pair * per + n
            if not isinstance(v, int) or v > 0:
                eng.wait_ge(s, v)

        def passes(hi_l, lo_l, hi_r, lo_r):
            return ((hi_l, hi_r), (hi_l, lo_r), (lo_l, hi_r))

        def steps(program):
            def run(eng):
                program(-1, False, True, True)
                program(0, True, True, True)
                with eng.Fori(1, PAIRS - 2) as i:
                    program(i, True, True, True)
                program(PAIRS - 2, True, True, False)
                program(PAIRS - 1, True, False, False)
            return run

        block = ctx.enter_context(nc.Block())

        @block.sync
        def _(sp):
            def load_x(p):
                for b in (0, 1):
                    sp.dma_start(x_in[:, b * T:(b + 1) * T, :].rearrange("p t d -> p (t d)"),
                                 x_rows[p, :, b, :]).then_inc(x_loaded, 16)

            def load_ctx(p, m):
                sp.dma_start(z2[:, m, :, :].rearrange("p (b t) d -> p b (t d)", b=2),
                             ctx_rows[m][p, :, :, :]).then_inc(ctx_loaded[m], 16)

            def load_res(p):
                for b in (0, 1):
                    sp.dma_start(x_res[:, b * T:(b + 1) * T, :].rearrange("p t d -> p (t d)"),
                                 x_rows[p, :, b, :]).then_inc(res_loaded, 16)

            def weight(dst, src, s):
                sp.dma_start(dst[:], src.rearrange("(c p) n -> p c n", p=P)).then_inc(s, 16)

            def row(dst, src, s):
                sp.dma_start(dst, src[None, :].to_broadcast([P, src.shape[0]])).then_inc(s, 16)

            weight(Wq[0], par(0, "Wq"), ld["Wq0"])
            weight(Wk[0], par(0, "Wk"), ld["Wk0"])
            load_x(0)
            for m in (0, 1):
                if m == 1:
                    weight(Wq[1], par(1, "Wq"), ld["Wq1"])
                    weight(Wk[1], par(1, "Wk"), ld["Wk1"])
                row(bq_row[:, m, :], par(m, "bq"), ld[f"b{m}"])
                row(bk_row[:, m, :], par(m, "bk"), ld[f"b{m}"])
            for m in (0, 1):
                load_ctx(0, m)
            for m in (0, 1):
                weight(Wv[m], par(m, "Wv"), ld[f"Wv{m}"])
                weight(Wo[m], par(m, "Wo"), ld[f"Wo{m}"])
            weight(fcW, a["L0_xattn_fc_W"], ld["fcW"])
            for m in (0, 1):
                row(bo[:, m, :], par(m, "bo"), ld["rows"])
            row(fcb[:], a["L0_xattn_fc_b"], ld["rows"])
            wait(sp, z1_ready, 0, 4, 4)
            load_x(1)
            sp.wait_ge(rows_full, 2)
            load_res(0)

            def body(i, back, front, norms):
                X, Y, Z = i, i + 1, i + 2
                if norms:
                    wait(sp, zc_full, Y, 4, 4)
                    wait(sp, z2r_lo_done, Y, 2, 2)
                    for m in (0, 1):
                        load_ctx(Z, m)
                    if not isinstance(i, int) or i + 3 < PAIRS:
                        wait(sp, z1_ready, Z, 4, 4)
                        load_x(i + 3)
                if back:
                    if front:
                        wait(sp, y_ready, X, 4, 4)
                        load_res(Y)
                    for b in (0, 1):
                        wait(sp, out_ready, X, 4, (b + 1) * T)
                        sp.dma_start(out_rows[X, :, b, :],
                                     y[:, b * T:(b + 1) * T, :].rearrange("p t d -> p (t d)")).then_inc(stored[b], 16)

            body(-1, False, True, True)
            body(0, True, True, True)
            with sp.Fori(1, PAIRS - 3) as i:
                body(i, True, True, True)
            body(PAIRS - 3, True, True, True)
            body(PAIRS - 2, True, True, False)
            body(PAIRS - 1, True, False, False)
            for b in (0, 1):
                sp.wait_ge(stored[b], 16 * PAIRS)

        @block.tensor
        def _(pe):
            def mm(out, l, r, start, stop):
                return nc.tensor.matmul(out, l, r, start=start, stop=stop)

            banks = [0]

            def turn_weight(src, rows):
                for e in range(EC):
                    k = banks[0]
                    if k >= 3:
                        pe.wait_ge(w_copied, k - 2)
                    for r in range(rows):
                        last = nc.tensor.transpose(turn[k % 3][:, r * P:(r + 1) * P],
                                                   src[:, r, e * P:(e + 1) * P], ident[:])
                    last.then_inc(w_turned, 1)
                    banks[0] += 1

            def product(k, l, chunks, n):
                bank = prod[2 + k % 2]
                if k >= 2:
                    pe.wait_ge(big_lo, k - 1)
                for e in range(EC):
                    last = mm(bank[:, 0:n], l(e), chunks(e), e == 0, e == EC - 1)
                last.then_inc(big_full, 1)

            def w_broadcast(m):
                pe.wait_ge(diag_ready, m + 1)
                if m == 1:
                    pe.wait_ge(w_row_ready, 1)
                mm(turn[3][:], ones[:], scratch[:], True, True).then_inc(w_row_full, 1)

            pe.wait_ge(ident_ready, 1)
            for m in (0, 1):
                pe.wait_ge(ld[f"Wq{m}"], 16)
                turn_weight(Wq[m], DC)
                if m == 0:
                    pe.wait_ge(vec_loaded, 16 * len(vec_at))
                    nc.tensor.transpose(turn[3][:, 0:NVEC], vec_rows[0:NVEC, :],
                                        ident[0:NVEC, 0:NVEC]).then_inc(vec_turned, 1)
                pe.wait_ge(b_rep_ready, m + 1)
                if m == 1:
                    pe.wait_ge(qk_rows_sb, 2)
                for c in range(DC):
                    mm(prod[0][:], b1_rep[:, m, c, :], Wq[m][:, c, :], c == 0, c == DC - 1)
                pe.wait_ge(ld[f"Wk{m}"], 16)
                for c in range(D2C):
                    last = mm(prod[1][:], b2_rep[:, m, c, :], Wk[m][:, c, :], c == 0, c == D2C - 1)
                last.then_inc(qk_rows, 1)
                pe.wait_ge(wkg_ready, m + 1)
                turn_weight(Wkg[m], D2C)
                pe.wait_ge(w_copied, banks[0])
                if m == 1:
                    w_broadcast(0)
                for j in range(DC):
                    product(m * DC + j, lambda e: WqT[m][:, e, j * P:(j + 1) * P], lambda e: WkT[m][:, e, :], D2)
            w_broadcast(1)
            for m in (0, 1):
                pe.wait_ge(ld[f"Wv{m}"], 16)
                if m == 0:
                    pe.wait_ge(qk_rows_sb, 4)
                for e in range(EC):
                    for c in range(D2C):
                        last = mm(prod[m][:, e:e + 1], Wv[m][:, c, e * P:(e + 1) * P],
                                  v_(m, "ln2_b", c), c == 0, c == D2C - 1)
                last.then_inc(bv_cols, 1)
                turn_weight(Wv[m], D2C)
            for m in (0, 1):
                pe.wait_ge(w_copied, banks[0] - 4 * (1 - m))
                pe.wait_ge(ld[f"Wo{m}"], 16)
                for j in range(D2C):
                    product(2 * DC + m * D2C + j, lambda e: WvT[m][:, e, j * P:(j + 1) * P],
                            lambda e: Wo[m][:, e, :], D)
            pe.wait_ge(bv_rep_ready, 2)
            for m in (0, 1):
                for e in range(EC):
                    last = mm(prod[0][:], bv_rep[:, m, e, :], Wo[m][:, e, :], (m, e) == (0, 0), (m, e) == (1, EC - 1))
            last.then_inc(rows_full, 1)
            pe.wait_ge(ld["fcW"], 16)
            pe.wait_ge(ln_rep_ready, 1)
            for c in range(DC):
                last = mm(prod[1][:], ln_b_rep[:, c, :], fcW[:, c, :], c == 0, c == DC - 1)
            last.then_inc(rows_full, 1)
            pe.wait_ge(rows_ready, 2)
            pe.wait_ge(w_row_ready, 2)
            pe.wait_ge(big_lo, 2 * DC + 2 * D2C)

            def body(i, back, front, norms):
                X, Y = i, i + 1

                def turn_z1(k):
                    if k == 0:
                        wait(pe, z1_ready, Y, 4, 4)
                    wait(pe, pt_lo, X, 4, k + 1)
                    for n in range(TILES):
                        last = nc.tensor.transpose(turn[k][:, n * P:(n + 1) * P], z1[:, n, k * P:(k + 1) * P], ident[:])
                    last.then_inc(zx_full, 1)

                def context(k):
                    b, m = divmod(k, 2)
                    wait(pe, pt_lo, X, 4, k + 1)
                    wait(pe, out_ready, X - 1, 4, k + 1)
                    if b == 0:
                        wait(pe, z2r_lo_done, X, 2, m + 1)
                    for j in range(D2C):
                        for kt in range(T):
                            l = (z2r_hi[:, m, b * T + kt, j * P:(j + 1) * P], z2r_lo[:, m, b * T + kt, j * P:(j + 1) * P])
                            r = (share_hi[:, k, kt * S:(kt + 1) * S], share_lo[:, k, kt * S:(kt + 1) * S])
                            for q, (ll, rr) in enumerate(passes(*l, *r)):
                                last = mm(prod[k][:, j * S:(j + 1) * S], ll, rr, kt == 0 and q == 0,
                                          kt == T - 1 and q == 2)
                    last.then_inc(c_full, 1)

                def project(k):
                    m, j = divmod(k, D2C)
                    if back:
                        wait(pe, c_lo, X, 4, k + 1)
                    for c in range(DC):
                        if k == 0:
                            wait(pe, zx_lo, Y, 4, c + 1)
                        l = (M_hi[:, m, c, j * P:(j + 1) * P], M_lo[:, m, c, j * P:(j + 1) * P])
                        for q, (ll, rr) in enumerate(passes(*l, z1T_hi[:, c, :], z1T_lo[:, c, :])):
                            last = mm(prod[k][:], ll, rr, c == 0 and q == 0, c == DC - 1 and q == 2)
                    last.then_inc(t_full, 1)

                def turn_z2(k):
                    m, j = divmod(k, D2C)
                    wait(pe, z2_ready, Y, 8, 4 * m + 4)
                    wait(pe, zx_lo, Y, 4, k + 1)
                    for n in range(TILES):
                        last = nc.tensor.transpose(turn[k][:, n * P:(n + 1) * P], z2[:, m, n, j * P:(j + 1) * P], ident[:])
                    last.then_inc(zc_full, 1)

                def output(n):
                    b, t = divmod(n, T)
                    if t == 0:
                        wait(pe, c_lo, X, 4, 2 * b + 2)
                    if front:
                        wait(pe, t_lo, Y, 4, n + 1)
                    for m in (0, 1):
                        for j in range(D2C):
                            l = (cT_hi[:, b, m, j, t * P:(t + 1) * P], cT_lo[:, b, m, j, t * P:(t + 1) * P])
                            for q, (ll, rr) in enumerate(passes(*l, WA_hi[:, m, j, :], WA_lo[:, m, j, :])):
                                last = mm(prod[n][:], ll, rr, (m, j, q) == (0, 0, 0), (m, j, q) == (1, D2C - 1, 2))
                    last.then_inc(f_full, 1)

                def scores(k):
                    b, m = divmod(k, 2)
                    if k < 2:
                        wait(pe, t_lo, Y, 4, 2 * m + 2)
                        wait(pe, zc_lo, Y, 4, 2 * m + 2)
                    if back:
                        wait(pe, y_ready, X, 4, k + 1)
                    for t in range(T):
                        n = b * T + t
                        for j in range(D2C):
                            l = (tT_hi[:, m, j, n * P:(n + 1) * P], tT_lo[:, m, j, n * P:(n + 1) * P])
                            r = (z2T_hi[:, m, j, b * S:(b + 1) * S], z2T_lo[:, m, j, b * S:(b + 1) * S])
                            for q, (ll, rr) in enumerate(passes(*l, *r)):
                                last = mm(prod[k][:, t * S:(t + 1) * S], ll, rr, j == 0 and q == 0,
                                          j == D2C - 1 and q == 2)
                    last.then_inc(s_full, 1)

                def turn_y(n):
                    wait(pe, yn_ready, X, 4, n + 1)
                    if front:
                        wait(pe, zc_lo, Y, 4, n + 1)
                    for c in range(DC):
                        last = nc.tensor.transpose(turn[n][:, c * P:(c + 1) * P], yn[:, n % 2, c * P:(c + 1) * P], ident[:])
                    last.then_inc(yt_full, 1)

                def linear(n):
                    wait(pe, yt_lo, X, 4, n + 1)
                    if front:
                        wait(pe, exp_done, Y, 8, 2 * n + 2)
                    for c in range(DC):
                        l = (share_hi[:, n, c * P:(c + 1) * P], share_lo[:, n, c * P:(c + 1) * P])
                        for q, (ll, rr) in enumerate(passes(*l, fc_hi[:, c, :], fc_lo[:, c, :])):
                            last = mm(prod[n][:], ll, rr, c == 0 and q == 0, c == DC - 1 and q == 2)
                    last.then_inc(h_full, 1)

                def turn_probs(k):
                    b, m = divmod(k, 2)
                    wait(pe, probs_ready, Y, 8, 2 * k + 2)
                    if back:
                        wait(pe, yt_lo, X, 4, k + 1)
                    else:
                        wait(pe, zc_lo, Y, 4, k + 1)
                    for kt in range(T):
                        for t in range(T):
                            last = nc.tensor.transpose(turn[k][:, kt * S + t * P:kt * S + (t + 1) * P],
                                                       probs[:, b, m, t, kt * P:(kt + 1) * P], ident[:])
                    last.then_inc(pt_full, 1)

                for k in range(4):
                    if front:
                        turn_z1(k)
                    if back:
                        context(k)
                if front:
                    for k in range(4):
                        project(k)
                        turn_z2(k)
                for n in range(4):
                    if back:
                        output(n)
                        if n >= 2:
                            turn_y(n - 2)
                for k in range(4):
                    if front:
                        scores(k)
                    if back and k < 2:
                        turn_y(k + 2)
                for n in range(4):
                    if back:
                        linear(n)
                    if front and n > 0:
                        turn_probs(n - 1)
                if front:
                    turn_probs(3)

            steps(body)(pe)

        @block.scalar
        def _(act):
            def hi(out, in_, **kw):
                return nc.scalar.activation(out, in_, ACT.Identity if "bias" in kw else ACT.Copy, **kw)

            for key, (at, c) in vec_at.items():
                src = par(*key) if isinstance(key, tuple) else a["L0_xattn_" + key]
                act.dma_start(vec_rows[at:at + c, :], src.rearrange("(c p) -> c p", p=P)).then_inc(vec_loaded, 16)
            banks = [0]

            def copy_turned(dst, rows):
                for e in range(EC):
                    act.wait_ge(w_turned, banks[0] + 1)
                    nc.scalar.copy(dst[:, e, :], turn[banks[0] % 3][:, 0:rows * P]).then_inc(w_copied, 1)
                    banks[0] += 1

            for m in (0, 1):
                copy_turned(WqT[m], DC)
                copy_turned(WkT[m], D2C)
                act.wait_ge(g1s_ready, m + 1)
                for j in range(DC):
                    k = m * DC + j
                    act.wait_ge(big_full, k + 1)
                    hi(M_hi[:, m, j, :], prod[2 + k % 2][:, 0:D2], scale=col(G1S, m, j, j + 1)).then_inc(big_hi, 1)
            for m in (0, 1):
                copy_turned(WvT[m], D2C)
            for m in (0, 1):
                for j in range(D2C):
                    k = 2 * DC + m * D2C + j
                    act.wait_ge(big_full, k + 1)
                    hi(WA_hi[:, m, j, :], prod[2 + k % 2][:], scale=v_(m, "ln2_g", j)).then_inc(big_hi, 1)
            act.wait_ge(ld["fcW"], 16)
            for c in range(DC):
                g = vec_at["ln_g"][0] + c
                hi(fc_hi[:, c, :], fcW[:, c, :], scale=vec[:, g:g + 1]).then_inc(fc_hi_done, 1)

            def body(i, back, front, norms):
                X, Y = i, i + 1

                def sum_product(k):
                    n, m = divmod(k, 2)
                    slot = probs[:, k % 4 // 2, k % 2, :, :].rearrange("p t s -> p (t s)")
                    wait(act, r_product, Y, 8, k + 1)
                    nc.scalar.activation(slot, slot, ACT.Copy, accum_out=r_sum[:, n, m:m + 1]).then_inc(r_summed, 1)

                def hi_y(n):
                    wait(act, yt_full, X, 4, n + 1)
                    hi(share_hi[:, n, :], turn[n][:]).then_inc(yt_hi, 1)

                def exp(k):
                    b, m = divmod(k, 2)
                    wait(act, bias_ready, Y, 4, k + 1)
                    for t in range(T):
                        nc.scalar.activation(probs[:, b, m, t, :], prod[k][:, t * S:(t + 1) * S], ACT.Exp,
                                             bias=exp_bias[:, b, m, t:t + 1],
                                             accum_out=exp_sum[:, b, m, t:t + 1]).then_inc(exp_done, 1)

                def normalise(k):
                    b, m = divmod(k, 2)
                    wait(act, inv_ready, Y, 4, k + 1)
                    for t in range(T):
                        nc.scalar.activation(probs[:, b, m, t, :], probs[:, b, m, t, :], ACT.Copy,
                                             scale=exp_inv[:, b, m, t:t + 1]).then_inc(probs_ready, 1)

                for k in range(4):
                    if front:
                        wait(act, zx_full, Y, 4, k + 1)
                        hi(z1T_hi[:, k, :], turn[k][:]).then_inc(zx_hi, 1)
                    if back:
                        b, m = divmod(k, 2)
                        wait(act, c_full, X, 4, k + 1)
                        hi(cT_hi[:, b, m, :, :].rearrange("p j s -> p (j s)"), prod[k][:]).then_inc(c_hi, 1)
                    if front and k >= 2:
                        sum_product(2 * k - 4)
                        sum_product(2 * k - 3)
                if front:
                    for k in range(4):
                        m, j = divmod(k, D2C)
                        if j == 0:
                            wait(act, z2_ready, Y, 8, 4 * m + 4)
                            hi(z2r_hi[:, m, :, :].rearrange("p n d -> p (n d)"),
                               z2[:, m, :, :].rearrange("p n d -> p (n d)")).then_inc(z2r_hi_done, 1)
                        wait(act, t_full, Y, 4, k + 1)
                        hi(tT_hi[:, m, j, :], prod[k][:], bias=u_col[:, m, j:j + 1]).then_inc(t_hi, 1)
                        wait(act, zc_full, Y, 4, k + 1)
                        hi(z2T_hi[:, m, j, :], turn[k][:]).then_inc(zc_hi, 1)
                        sum_product(k + 4)
                if back:
                    for n in range(3):
                        hi_y(n)
                if front:
                    exp(0)
                if back:
                    hi_y(3)
                if front:
                    exp(1)
                    normalise(0)
                    exp(2)
                    normalise(1)
                    exp(3)
                    normalise(2)
                    normalise(3)
                    for k in range(4):
                        wait(act, pt_full, Y, 4, k + 1)
                        hi(share_hi[:, k, :], turn[k][:]).then_inc(pt_hi, 1)

            steps(body)(act)

        @block.vector
        def _(dve):
            def lo(out, in_, h):
                return nc.vector.tensor_tensor(out, in_, h.bitcast(F32), ALU.subtract)

            def lo_scaled(out, in_, s, h):
                return nc.vector.scalar_tensor_tensor(out, in_, s, h.bitcast(F32), ALU.mult, ALU.subtract)

            def x_bn_stats(p):
                wait(dve, x_loaded, p, 32, 32)
                for n in range(TILES):
                    nc.vector.bn_stats(x_bn[:, n, :], x_in[:, n, :]).then_inc(x_bn_done, 1)

            def x_bn_wait(p):
                wait(dve, x_bn_done, p, 4, 4)

            def x_bn_aggr():
                for n in range(TILES):
                    nc.vector.bn_aggr(x_mv[:, n, :], x_bn[:, n, :]).then_inc(x_stats, 1)

            def norm_x(p, n):
                wait(dve, x_rstd_done, p, 1, 1)
                nc.vector.tensor_scalar(z1[:, n, :], x_in[:, n, :], x_mv[:, n, 0:1], x_rstd[:, n:n + 1],
                                        ALU.subtract, ALU.mult).then_inc(z1_ready, 1)

            def ctx_bn_stats(p, m):
                wait(dve, ctx_loaded[m], p, 16, 16)
                for n in range(TILES):
                    nc.vector.bn_stats(ctx_bn[:, m, n, :], z2[:, m, n, :]).then_inc(ctx_bn_done, 1)

            def ctx_bn_wait(p, m):
                wait(dve, ctx_bn_done, p, 8, 4 * m + 4)

            def ctx_bn_aggr(m):
                for n in range(TILES):
                    nc.vector.bn_aggr(ctx_mv[:, m, n, :], ctx_bn[:, m, n, :]).then_inc(ctx_stats, 1)

            def norm_ctx(p, m):
                wait(dve, ctx_rstd_done, p, 2, m + 1)
                for n in range(TILES):
                    nc.vector.tensor_scalar(z2[:, m, n, :], z2[:, m, n, :], ctx_mv[:, m, n, 0:1],
                                            ctx_rstd[:, m, n:n + 1], ALU.subtract, ALU.mult).then_inc(z2_ready, 1)

            def repeat(dst, src, chunks):
                for c in range(chunks):
                    last = nc.vector.tensor_scalar(dst[:, c, :], ones[:], src[:, c:c + 1], None, ALU.mult)
                return last

            DOTS = D2C + DC + 1

            def dot(k, out, l, r):
                if k:
                    dve.wait_ge(dots, k)
                nc.vector.tensor_tensor_reduce(scratch[:], l, r, 1.0, 0.0, ALU.mult, ALU.add, out).then_inc(dots, 1)

            def vec_cols(key):
                at, c = vec_at[key]
                return vec[:, at:at + c]

            def take_w_row(m):
                dve.wait_ge(w_row_full, m + 1)
                nc.vector.tensor_copy(w_row[:, m, :], turn[3][:]).then_inc(w_row_ready, 1)

            nc.vector.memset(ones[:], 1.0).then_inc(ones_ready, 1)
            dve.wait_ge(vec_turned, 1)
            nc.vector.tensor_copy(vec[:, 0:NVEC], turn[3][:, 0:NVEC]).then_inc(vec_ready, 1)
            dve.wait_ge(vec_ready, 1)
            dve.wait_ge(ones_ready, 1)
            for m in (0, 1):
                repeat(b1_rep[:, m], vec_cols((m, "ln1_b")), DC)
                repeat(b2_rep[:, m], vec_cols((m, "ln2_b")), D2C).then_inc(b_rep_ready, 1)
                nc.vector.tensor_scalar(col(G1S, m, 0, 4), vec_cols((m, "ln1_g")), SCALE, None,
                                        ALU.mult).then_inc(g1s_ready, 1)
            for m in (0, 1):
                dve.wait_ge(ld[f"Wk{m}"], 16)
                for c in range(D2C):
                    last = nc.vector.tensor_scalar(Wkg[m][:, c, :], Wk[m][:, c, :], v_(m, "ln2_g", c), None, ALU.mult)
                last.then_inc(wkg_ready, 1)
                if m == 0:
                    x_bn_stats(0)
                    x_bn_wait(0)
                    x_bn_aggr()
                dve.wait_ge(qk_rows, m + 1)
                dve.wait_ge(ld[f"b{m}"], 32)
                nc.vector.tensor_tensor(bq_row[:, m, :], prod[0][:], bq_row[:, m, :], ALU.add).then_inc(qk_rows_sb, 1)
                nc.vector.tensor_tensor(bk_row[:, m, :], prod[1][:], bk_row[:, m, :], ALU.add).then_inc(qk_rows_sb, 1)
                if m == 0:
                    for n in range(TILES):
                        norm_x(0, n)
                dve.wait_ge(qk_rows_sb, 2 * m + 2)
                dve.wait_ge(wkg_ready, m + 1)
                if m == 1:
                    take_w_row(0)
                for j in range(D2C):
                    dot(m * DOTS + j, u_col[:, m, j:j + 1], Wkg[m][:, j, :], bq_row[:, m, :])
                for j in range(DC):
                    dot(m * DOTS + D2C + j, col(WB, m, j, j + 1), Wq[m][:, j, :], bk_row[:, m, :])
                dot(m * DOTS + D2C + DC, r0[:, 0, m:m + 1], bq_row[:, m, :], bk_row[:, m, :])
                for j in range(DC):
                    k = m * DC + j
                    dve.wait_ge(big_hi, k + 1)
                    lo_scaled(M_lo[:, m, j, :], prod[2 + k % 2][:, 0:D2], col(G1S, m, j, j + 1),
                              M_hi[:, m, j, :]).then_inc(big_lo, 1)
                dve.wait_ge(dots, (m + 1) * DOTS)
                nc.vector.tensor_tensor(col(W, m, 0, 4), col(WB, m, 0, 4), col(G1S, m, 0, 4),
                                        ALU.mult).then_inc(w_col_ready, 1)
                nc.vector.tensor_scalar(u_col[:, m, :], u_col[:, m, :], SCALE, None, ALU.mult)
                for n in reversed(range(TILES)):
                    nc.vector.tensor_scalar(r0[:, n, m:m + 1], r0[:, 0, m:m + 1], SCALE, None, ALU.mult)
                dve.wait_ge(w_col_ready, m + 1)
                for c in range(DC):
                    last = nc.vector.tensor_scalar(scratch[:, c * P:(c + 1) * P], ident[:], col(W, m, c, c + 1), None,
                                                   ALU.mult)
                last.then_inc(diag_ready, 1)
                if m == 0:
                    repeat(ln_b_rep, vec_cols("ln_b"), DC).then_inc(ln_rep_ready, 1)
                    for mm_ in (0, 1):
                        ctx_bn_stats(0, mm_)
                        ctx_bn_wait(0, mm_)
                        ctx_bn_aggr(mm_)
            for m in (0, 1):
                norm_ctx(0, m)
            take_w_row(1)
            for m in (0, 1):
                dve.wait_ge(bv_cols, m + 1)
                nc.vector.tensor_tensor(col(BV, m, 0, 4), prod[m][:, 0:4], vec_cols((m, "bv")),
                                        ALU.add).then_inc(bv_ready, 1)
                dve.wait_ge(bv_ready, m + 1)
                repeat(bv_rep[:, m], col(BV, m, 0, 4), EC).then_inc(bv_rep_ready, 1)
            for m in (0, 1):
                for j in range(D2C):
                    k = 2 * DC + m * D2C + j
                    dve.wait_ge(big_hi, k + 1)
                    lo_scaled(WA_lo[:, m, j, :], prod[2 + k % 2][:], v_(m, "ln2_g", j), WA_hi[:, m, j, :]).then_inc(big_lo, 1)
            dve.wait_ge(ld["rows"], 48)
            nc.vector.tensor_tensor(bo[:, 0, :], bo[:, 0, :], bo[:, 1, :], ALU.add).then_inc(bo_summed, 1)
            for c in range(DC):
                g = vec_at["ln_g"][0] + c
                dve.wait_ge(fc_hi_done, c + 1)
                lo_scaled(fc_lo[:, c, :], fcW[:, c, :], vec[:, g:g + 1], fc_hi[:, c, :]).then_inc(fc_lo_done, 1)
            dve.wait_ge(bo_summed, 1)
            dve.wait_ge(rows_full, 1)
            nc.vector.tensor_tensor(c_row[:], prod[0][:], bo[:, 0, :], ALU.add).then_inc(rows_ready, 1)
            dve.wait_ge(rows_full, 2)
            nc.vector.tensor_tensor(f_row[:], prod[1][:], fcb[:], ALU.add).then_inc(rows_ready, 1)

            def body(i, back, front, norms):
                X, Y, Z = i, i + 1, i + 2
                for k in range(4):
                    if front:
                        wait(dve, zx_hi, Y, 4, k + 1)
                        lo(z1T_lo[:, k, :], turn[k][:], z1T_hi[:, k, :]).then_inc(zx_lo, 1)
                    if back:
                        b, m = divmod(k, 2)
                        wait(dve, c_hi, X, 4, k + 1)
                        lo(cT_lo[:, b, m, :, :].rearrange("p j s -> p (j s)"), prod[k][:],
                           cT_hi[:, b, m, :, :].rearrange("p j s -> p (j s)")).then_inc(c_lo, 1)
                if norms:
                    x_bn_stats(Z)
                if front:
                    for k in range(4):
                        m, j = divmod(k, D2C)
                        wait(dve, t_hi, Y, 4, k + 1)
                        if norms and k == 0:
                            x_bn_wait(Z)
                        nc.vector.scalar_tensor_tensor(tT_lo[:, m, j, :], prod[k][:], u_col[:, m, j:j + 1],
                                                       tT_hi[:, m, j, :].bitcast(F32), ALU.add,
                                                       ALU.subtract).then_inc(t_lo, 1)
                        if norms and k == 0:
                            x_bn_aggr()
                        wait(dve, zc_hi, Y, 4, k + 1)
                        lo(z2T_lo[:, m, j, :], turn[k][:], z2T_hi[:, m, j, :]).then_inc(zc_lo, 1)
                if norms:
                    wait(dve, r_product, Y, 8, 8)
                    for n in range(TILES - back):
                        norm_x(Z, n)

                def norm_y(n):
                    wait(dve, y_rstd_done, X, 4, n + 1)
                    if n >= 2:
                        wait(dve, yt_full, X, 4, n - 1)
                    nc.vector.tensor_scalar(yn[:, n % 2, :], y[:, n, :], y_mv[:, n, 0:1], y_rstd[:, n:n + 1],
                                            ALU.subtract, ALU.mult).then_inc(yn_ready, 1)

                def lo_y(n):
                    wait(dve, yt_hi, X, 4, n + 1)
                    lo(share_lo[:, n, :], turn[n][:], share_hi[:, n, :]).then_inc(yt_lo, 1)

                def invert(k):
                    b, m = divmod(k, 2)
                    wait(dve, exp_done, Y, 8, 2 * k + 2)
                    nc.vector.reciprocal(exp_inv[:, b, m, :], exp_sum[:, b, m, :]).then_inc(inv_ready, 1)

                def row_max(k):
                    b, m = divmod(k, 2)
                    wait(dve, s_full, Y, 4, k + 1)
                    nc.vector.tensor_reduce(neg_max[:, b, m, :], prod[k][:].rearrange("p (t s) -> p t s", t=T),
                                            AX_X, ALU.max, negate=True).then_inc(max_ready, 1)

                if back:
                    for n in range(4):
                        wait(dve, f_full, X, 4, n + 1)
                        wait(dve, res_ready, X, 4, n + 1)
                        wait(dve, stored[n // T], X - 1, 16, 16)
                        nc.vector.tensor_tensor(y[:, n, :], prod[n][:], x_res[:, n, :], ALU.add).then_inc(y_ready, 1)
                        if n >= 2:
                            lo_y(n - 2)
                        wait(dve, y_ready, X, 4, n + 1)
                        nc.vector.bn_stats(y_bn[:, n, :], y[:, n, :]).then_inc(y_bn_done, 1)
                        wait(dve, y_bn_done, X, 4, n + 1)
                        if n == 0 and norms:
                            norm_x(Z, TILES - 1)
                        if n > 0:
                            norm_y(n - 1)
                        nc.vector.bn_aggr(y_mv[:, n, :], y_bn[:, n, :]).then_inc(y_stats, 1)
                if front:
                    row_max(0)
                if back:
                    norm_y(3)
                    lo_y(2)
                if front:
                    row_max(1)
                if back:
                    lo_y(3)
                if front:
                    invert(0)
                    row_max(2)
                    invert(1)
                    row_max(3)
                for n in range(4):
                    if norms and n < 2:
                        ctx_bn_stats(Z, n)
                        ctx_bn_wait(Z, n)
                    if front and n < 2:
                        invert(n + 2)
                    if back:
                        wait(dve, h_full, X, 4, n + 1)
                        wait(dve, yf_ready, X, 4, n + 1)
                        nc.vector.tensor_tensor(y[:, n, :], prod[n][:], y[:, n, :], ALU.add).then_inc(out_ready, 1)
                    if norms:
                        if n < 2:
                            ctx_bn_aggr(n)
                        else:
                            norm_ctx(Z, n - 2)
                    if front and n > 0:
                        wait(dve, pt_hi, Y, 4, n)
                        lo(share_lo[:, n - 1, :], turn[n - 1][:], share_hi[:, n - 1, :]).then_inc(pt_lo, 1)
                if front:
                    wait(dve, pt_hi, Y, 4, 4)
                    lo(share_lo[:, 3, :], turn[3][:], share_hi[:, 3, :]).then_inc(pt_lo, 1)

            steps(body)(dve)

        @block.gpsimd
        def _(pool):
            nc.gpsimd.memset(ident[:], 0.0).then_inc(zeroed, 1)
            pool.wait_ge(zeroed, 1)
            nc.gpsimd.affine_select(out=ident[:], in_=ident[:], compare_op=ALU.not_equal, fill=1.0, base=0,
                                    pattern=[[-1, P]], channel_multiplier=1).then_inc(ident_ready, 1)
            nc.gpsimd.memset(minus_half[:], -0.5).then_inc(zeroed, 1)
            nc.gpsimd.memset(eps[:], EPS).then_inc(zeroed, 1)
            pool.wait_ge(zeroed, 3)

            def rstd(ve, out, mv, width, stats, stats_at, ve_done, ve_at, done):
                wait(pool, stats, *stats_at)
                nc.gpsimd.tensor_tensor(ve, mv, eps[:, 0:width], ALU.add).then_inc(ve_done, 1)
                wait(pool, ve_done, *ve_at)
                nc.gpsimd.tensor_tensor(out, ve, minus_half[:, 0:width], ALU.pow).then_inc(done, 1)

            def rstd_x(p):
                rstd(x_ve[:], x_rstd[:], x_mv[:, :, 1], TILES, x_stats, (p, 4, 4), x_ve_done, (p, 1, 1), x_rstd_done)

            def rstd_ctx(p, m):
                rstd(ctx_ve[:, m, :], ctx_rstd[:, m, :], ctx_mv[:, m, :, 1], TILES, ctx_stats, (p, 8, 4 * m + 4),
                     ctx_ve_done, (p, 2, m + 1), ctx_rstd_done)

            rstd_x(0)
            rstd_ctx(0, 0)
            rstd_ctx(0, 1)

            pool.wait_ge(w_row_ready, 2)

            def body(i, back, front, norms):
                X, Y, Z = i, i + 1, i + 2
                if front:
                    wait(pool, z1_ready, Y, 4, 4)
                    for k in range(2 * TILES):
                        n, m = divmod(k, 2)
                        if k < 4:
                            wait(pool, pt_full, X, 4, k + 1)
                        else:
                            wait(pool, r_summed, Y, 8, k - 3)
                        nc.gpsimd.tensor_tensor(probs[:, k % 4 // 2, k % 2, :, :].rearrange("p t s -> p (t s)"),
                                                z1[:, n, :], w_row[:, m, :], ALU.mult).then_inc(r_product, 1)
                if back:
                    wait(pool, res_loaded, X, 32, 32)
                    if isinstance(i, int) and i == 0:
                        pool.wait_ge(rows_ready, 2)
                    for n in range(TILES):
                        nc.gpsimd.tensor_tensor(x_res[:, n, :], x_res[:, n, :], c_row[:], ALU.add).then_inc(res_ready, 1)
                if norms:
                    rstd_x(Z)
                if front:
                    for m in (0, 1):
                        wait(pool, z2r_hi_done, Y, 2, m + 1)
                        nc.gpsimd.tensor_tensor(z2r_lo[:, m, :, :].rearrange("p n d -> p (n d)"),
                                                z2[:, m, :, :].rearrange("p n d -> p (n d)"),
                                                z2r_hi[:, m, :, :].rearrange("p n d -> p (n d)").bitcast(F32),
                                                ALU.subtract).then_inc(z2r_lo_done, 1)
                if back:
                    for n in range(TILES):
                        rstd(y_ve[:, n:n + 1], y_rstd[:, n:n + 1], y_mv[:, n, 1:2], 1, y_stats, (X, 4, n + 1),
                             y_ve_done, (X, 4, n + 1), y_rstd_done)
                if front:
                    wait(pool, r_summed, Y, 8, 8)
                    nc.gpsimd.tensor_tensor(r_sb[:], r_sum[:], r0[:], ALU.add).then_inc(r_ready, 1)
                    wait(pool, r_ready, Y, 1, 1)
                    for k in range(4):
                        b, m = divmod(k, 2)
                        wait(pool, max_ready, Y, 4, k + 1)
                        r = r_sb[:, b * T:(b + 1) * T, m]
                        nc.gpsimd.tensor_tensor(neg_top[:, b, m, :], neg_max[:, b, m, :], r, ALU.subtract).then_inc(top_ready, 1)
                        wait(pool, top_ready, Y, 4, k + 1)
                        nc.gpsimd.tensor_tensor(exp_bias[:, b, m, :], neg_top[:, b, m, :], r, ALU.add).then_inc(bias_ready, 1)
                if back:
                    for n in range(TILES):
                        wait(pool, yn_ready, X, 4, n + 1)
                        nc.gpsimd.tensor_tensor(y[:, n, :], y[:, n, :], f_row[:], ALU.add).then_inc(yf_ready, 1)
                if norms:
                    for m in (0, 1):
                        rstd_ctx(Z, m)

            steps(body)(pool)


def kernel(**inputs):
    import numpy as _np
    import concourse.bacc as _bacc
    from concourse import mybir as _mybir
    from concourse.bass_utils import run_bass_kernel_spmd as _run

    nc = _bacc.Bacc("TRN2", target_bir_lowering=False, num_devices=1)
    arrays, aps = {}, {}
    for name, value in inputs.items():
        v = _np.ascontiguousarray(value)
        arrays[f"in_{name}_dram"] = v
        aps[name] = nc.dram_tensor(f"in_{name}_dram", v.shape, _mybir.dt.from_np(v.dtype), kind="ExternalInput").ap()
    aps["out"] = nc.dram_tensor("out_0_dram", inputs["x"].shape, _mybir.dt.float32, kind="ExternalOutput").ap()
    build(nc, aps)
    r = _run(nc, [arrays], core_ids=[0])
    return r.results[0]["out_0_dram"]
```

```python
from contextlib import ExitStack

import concourse.bass as bass
from concourse import mybir

F32 = mybir.dt.float32
F32R = mybir.dt.float32r
ALU = mybir.AluOpType
ACT = mybir.ActivationFunctionType
AX_X = mybir.AxisListType.X
P = 128
EPS = 1e-5
MODS = ("a", "v")
VECTORS = [((m, n), f"L0_xattn_{MODS[m]}_{n}") for m in (0, 1) for n in ("ln1_g", "ln2_g", "ln2_b", "bq", "bk", "bv")]
VECTORS += [(n, f"L0_xattn_{n}") for n in ("ln_g", "ln_b")]


def build(nc, a):
    B, S, D = a["x"].shape
    D2 = a["ctx_512"].shape[2]
    E = a["L0_xattn_a_Wq"].shape[1]
    DC, EC, D2C = D // P, E // P, D2 // P
    T = S // P
    TILES = 2 * T
    PAIRS = B // 2
    ROWS = TILES * P
    SCALE = float(E) ** -0.5
    assert T == 2 and D2C == 2 and DC == 4 and EC == 4 and D == 512 and S == 256

    x_rows = a["x"].rearrange("(i b) (p t) d -> i p b (t d)", b=2, t=T)
    out_rows = a["out"].rearrange("(i b) (p t) d -> i p b (t d)", b=2, t=T)
    ctx_rows = [a[n].rearrange("(i b) (p t) d -> i p b (t d)", b=2, t=T)
                for n in ("ctx_512", "fside_BxSxS_0")]

    def par(m, name):
        return a[f"L0_xattn_{MODS[m]}_{name}"]

    ctx = ExitStack()
    with ctx:
        def sb(name, shape, dt=F32, stack=ctx):
            return stack.enter_context(nc.sbuf_tensor(name, shape, dt))

        def sem(name):
            return ctx.enter_context(nc.semaphore(name))

        prod = [ctx.enter_context(nc.psum_tensor(f"prod{k}", [P, 512], F32)) for k in range(4)]
        turn = [ctx.enter_context(nc.psum_tensor(f"turn{k}", [P, 512], F32)) for k in range(4)]

        M_hi = sb("M_hi", [P, 2, DC, D2], F32R)
        M_lo = sb("M_lo", [P, 2, DC, D2], F32R)
        WA_hi = sb("WA_hi", [P, 2, D2C, D], F32R)
        WA_lo = sb("WA_lo", [P, 2, D2C, D], F32R)
        fc_hi = sb("fc_hi", [P, DC, D], F32R)
        fc_lo = sb("fc_lo", [P, DC, D], F32R)
        c_row = sb("c_row", [P, D])
        f_row = sb("f_row", [P, D])
        ident = sb("ident", [P, P])
        ones = sb("ones", [P, P])
        vec = sb("vec", [P, 48])
        cols = sb("cols", [P, 36])
        u_col = sb("u_col", [P, 2, D2C])
        w_row = sb("w_row", [P, 2, D])
        r0 = sb("r0", [P, TILES, 2])
        r0_scratch = sb("r0_scratch", [P, 2, D2C + EC])
        one_128th = sb("one_128th", [P, 1])
        minus_half = sb("minus_half", [P, TILES])
        eps = sb("eps", [P, TILES])

        x_bn = sb("x_bn", [P, TILES, 6])
        x_mv = sb("x_mv", [P, TILES, 2])
        x_ve = sb("x_ve", [P, TILES])
        x_rstd = sb("x_rstd", [P, TILES])
        ctx_bn = sb("ctx_bn", [P, 2, TILES, 6])
        ctx_mv = sb("ctx_mv", [P, 2, TILES, 2])
        ctx_ve = sb("ctx_ve", [P, 2, TILES])
        ctx_rstd = sb("ctx_rstd", [P, 2, TILES])
        y_bn = sb("y_bn", [P, TILES, 6])
        y_mv = sb("y_mv", [P, TILES, 2])
        y_ve = sb("y_ve", [P, TILES])
        y_rstd = sb("y_rstd", [P, TILES])
        r_sum = sb("r_sum", [P, TILES, 2])
        r_sb = sb("r_sb", [P, TILES, 2])
        neg_max = sb("neg_max", [P, 2, 2, T])
        neg_top = sb("neg_top", [P, 2, 2, T])
        exp_bias = sb("exp_bias", [P, 2, 2, T])
        exp_sum = sb("exp_sum", [P, 2, 2, T])
        exp_inv = sb("exp_inv", [P, 2, 2, T])

        x_in = sb("x_in", [P, TILES, D])
        x_res = sb("x_res", [P, TILES, D])
        z1 = sb("z1", [P, TILES, D])
        z2 = sb("z2", [P, 2, TILES, D2])
        probs = sb("probs", [P, 2, 2, T, S])
        y = sb("y", [P, TILES, D])
        yn = sb("yn", [P, 2, D])

        first = ExitStack()
        WqT = [sb(f"WqT{m}", [P, EC, D], stack=first) for m in (0, 1)]
        w_diag = sb("w_diag", [P, 2, DC, P], stack=first)
        vec_rows = sb("vec_rows", [64, P], stack=first)
        w_scratch = sb("w_scratch", [P, D2 + 1], stack=first)
        norm_rows = sb("norm_rows", [P, 2, 2 * D + 2 * D2 + 1], stack=first)
        M_scaled = sb("M_scaled", [P, 2, DC, D2], stack=first)
        WkT = {m: sb(f"WkT{m}", [P, EC, D2 + 1], stack=first) for m in (1, 0)}
        first.close()
        z2r_hi = sb("z2r_hi", [P, 2, TILES, D2], F32R)
        z2r_lo = sb("z2r_lo", [P, 2, TILES, D2], F32R)
        z1T_hi = sb("z1T_hi", [P, DC, ROWS], F32R)
        z1T_lo = sb("z1T_lo", [P, DC, ROWS], F32R)
        z2T_hi = sb("z2T_hi", [P, 2, D2C, ROWS], F32R)
        z2T_lo = sb("z2T_lo", [P, 2, D2C, ROWS], F32R)
        tT_hi = sb("tT_hi", [P, 2, D2C, ROWS], F32R)
        tT_lo = sb("tT_lo", [P, 2, D2C, ROWS], F32R)

        second = ExitStack()
        bo_v = sb("bo_v", [P, D], stack=second)
        b2_rows = sb("b2_rows", [P, 2, D2], stack=second)
        scratch = sb("scratch", [P, D2], stack=second)
        fcW_b = sb("fcW_b", [P, DC, D], stack=second)
        Wo = [sb(f"Wo{m}", [P, EC, D], stack=second) for m in (0, 1)]
        second.close()
        WvT = [x_res[:, 2 * m:2 * m + 2, :].rearrange("p n d -> p (n d)").rearrange("p (c e) -> p c e", c=EC)
               for m in (0, 1)]
        fcW = y
        WA_f32 = yn
        WqT_b1 = [probs[:].rearrange("p b m t s -> p (b m t s)").rearrange("p (c e) -> p c e", c=EC), WqT[1]]
        cT_hi = sb("cT_hi", [P, 2, 2, D2C, S], F32R)
        cT_lo = sb("cT_lo", [P, 2, 2, D2C, S], F32R)
        share_hi = sb("share_hi", [P, 4, 512], F32R)
        share_lo = sb("share_lo", [P, 4, 512], F32R)

        vec_at, NVEC = {}, 0
        for key, name in VECTORS:
            vec_at[key] = (NVEC, a[name].shape[0] // P)
            NVEC += vec_at[key][1]

        def vec_cols(key):
            at, c = vec_at[key]
            return vec[:, at:at + c]

        def col(kind, m, k0=0, k1=4):
            at = (kind * 2 + m) * 4
            return cols[:, at + k0:at + k1]

        r0_cols = cols[:, 32:34]
        u_b2 = cols[:, 34:36]

        G1S, BQ, W, BV = range(4)
        b1_row, g1_row = [[norm_rows[:, m, k * D:(k + 1) * D] for m in (0, 1)] for k in (0, 1)]
        g2_row = [norm_rows[:, m, 2 * D:2 * D + D2] for m in (0, 1)]
        b2_one_row = [norm_rows[:, m, 2 * D + D2:2 * D + 2 * D2 + 1] for m in (0, 1)]

        ld = {k: sem(k + "_loaded") for k in ("vec", "WqT1", "WkT0", "WkT1", "WvT0", "WvT1", "Wo0", "Wo1", "b2_rows", "fc_b",
                                              "fcW", "norm_rows0", "norm_rows1", "rows")}
        ld["WqT0"] = [sem("WqT0_left_loaded"), sem("WqT0_right_loaded")]
        ld["WqT1"] = [ld["WqT1"]]
        zeroed = sem("zeroed")
        ident_ready = sem("ident_ready")
        ones_ready = sem("ones_ready")
        vec_turned = sem("vec_turned")
        vec_ready = sem("vec_ready")
        g1s_ready = sem("g1s_ready")
        products = sem("products")
        sums = sem("sums")
        bq_cols = sem("bq_cols")
        w_dots = sem("w_dots")
        diag_ready = sem("diag_ready")
        r0_parts = sem("r0_parts")
        r0_full = sem("r0_full")
        r0_ready = sem("r0_ready")
        dots = sem("dots")
        bv_ready = sem("bv_ready")
        rows_begun = sem("rows_begun")
        row_sums = sem("row_sums")
        f_parts = sem("f_parts")
        M_scaled_done = sem("M_scaled_done")
        M_full = sem("M_full")
        M_hi_done = sem("M_hi_done")
        M_lo_done = [sem("M_lo_done_a"), sem("M_lo_done_v")]
        w_full = sem("w_full")
        w_ready = sem("w_ready")
        u_full = sem("u_full")
        u_ready = sem("u_ready")
        WA_full = sem("WA_full")
        WA_hi_done = sem("WA_hi_done")
        WA_scaled = sem("WA_scaled")
        WA_lo_done = sem("WA_lo_done")
        rows_full = sem("rows_full")
        rows_ready = sem("rows_ready")
        fc_hi_done = sem("fc_hi_done")
        fc_lo_done = sem("fc_lo_done")

        x_loaded = sem("x_loaded")
        ctx_loaded = [sem("ctxa_loaded"), sem("ctxv_loaded")]
        res_loaded = sem("res_loaded")
        stored = [sem("stored0"), sem("stored1")]
        x_bn_done = sem("x_bn_done")
        x_stats = sem("x_stats")
        x_ve_done = sem("x_ve_done")
        x_rstd_done = sem("x_rstd_done")
        z1_ready = sem("z1_ready")
        ctx_bn_done = sem("ctx_bn_done")
        ctx_stats = sem("ctx_stats")
        ctx_ve_done = sem("ctx_ve_done")
        ctx_rstd_done = sem("ctx_rstd_done")
        z2_ready = sem("z2_ready")
        z2r_hi_done = sem("z2r_hi_done")
        z2r_lo_done = sem("z2r_lo_done")
        zx_full, zx_hi, zx_lo = sem("zx_full"), sem("zx_hi"), sem("zx_lo")
        zc_full, zc_hi, zc_lo = sem("zc_full"), sem("zc_hi"), sem("zc_lo")
        yt_full, yt_hi, yt_lo = sem("yt_full"), sem("yt_hi"), sem("yt_lo")
        pt_full, pt_hi, pt_lo = sem("pt_full"), sem("pt_hi"), sem("pt_lo")
        t_full, t_hi, t_lo = sem("t_full"), sem("t_hi"), sem("t_lo")
        c_full, c_hi, c_lo = sem("c_full"), sem("c_hi"), sem("c_lo")
        r_product = sem("r_product")
        r_summed = sem("r_summed")
        r_ready = sem("r_ready")
        s_full = sem("s_full")
        max_ready = sem("max_ready")
        top_ready = sem("top_ready")
        bias_ready = sem("bias_ready")
        exp_done = sem("exp_done")
        inv_ready = sem("inv_ready")
        probs_ready = sem("probs_ready")
        f_full = sem("f_full")
        res_ready = sem("res_ready")
        y_ready = sem("y_ready")
        y_bn_done = sem("y_bn_done")
        y_stats = sem("y_stats")
        y_ve_done = sem("y_ve_done")
        y_rstd_done = sem("y_rstd_done")
        yn_ready = sem("yn_ready")
        yf_ready = sem("yf_ready")
        h_full = sem("h_full")
        out_ready = sem("out_ready")

        def wait(eng, s, pair, per, n):
            v = pair * per + n
            if not isinstance(v, int) or v > 0:
                eng.wait_ge(s, v)

        def passes(hi_l, lo_l, hi_r, lo_r):
            return ((hi_l, hi_r), (hi_l, lo_r), (lo_l, hi_r))

        def steps(program):
            def run(eng):
                program(-1, False, True, True)
                program(0, True, True, True)
                with eng.Fori(1, PAIRS - 2) as i:
                    program(i, True, True, True)
                program(PAIRS - 2, True, True, False)
                program(PAIRS - 1, True, False, False)
            return run

        block = ctx.enter_context(nc.Block())

        @block.sync
        def _(sp):
            def load_x(p):
                for b in (0, 1):
                    sp.dma_start(x_in[:, b * T:(b + 1) * T, :].rearrange("p t d -> p (t d)"),
                                 x_rows[p, :, b, :]).then_inc(x_loaded, 16)

            def load_ctx(p, m):
                sp.dma_start(z2[:, m, :, :].rearrange("p (b t) d -> p b (t d)", b=2),
                             ctx_rows[m][p, :, :, :]).then_inc(ctx_loaded[m], 16)

            def load_res(p):
                for b in (0, 1):
                    sp.dma_start(x_res[:, b * T:(b + 1) * T, :].rearrange("p t d -> p (t d)"),
                                 x_rows[p, :, b, :]).then_inc(res_loaded, 16)

            def weight(dst, src, s):
                sp.dma_start(dst[:], src.rearrange("(c p) n -> p c n", p=P)).then_inc(s, 16)

            def row(dst, src, s):
                sp.dma_start(dst, src[None, :].to_broadcast([P, src.shape[0]])).then_inc(s, 16)

            sp.dma_start(vec_rows[0:NVEC, :], a["vectors"]).then_inc(ld["vec"], 16)
            weight(WkT[0], a["WkT0"], ld["WkT0"])
            for h in (0, 1):
                cols_h = slice(h * D // 2, (h + 1) * D // 2)
                sp.dma_start(WqT[0][:, :, cols_h],
                             a["WqT0"].rearrange("(c p) n -> p c n", p=P)[:, :, cols_h]).then_inc(ld["WqT0"][h], 16)
            row(norm_rows[:, 0, :], a["norm_rows"][0, :], ld["norm_rows0"])
            weight(WkT[1], a["WkT1"], ld["WkT1"])
            weight(WqT[1], a["WqT1"], ld["WqT1"][0])
            load_x(0)
            row(norm_rows[:, 1, :], a["norm_rows"][1, :], ld["norm_rows1"])
            for m in (0, 1):
                load_ctx(0, m)
            for m in (0, 1):
                weight(WvT[m], a[f"WvT{m}"], ld[f"WvT{m}"])
            for m in (0, 1):
                row(b2_rows[:, m, :], par(m, "ln2_b"), ld["b2_rows"])
            row(f_row[:], a["L0_xattn_fc_b"], ld["fc_b"])
            weight(fcW, a["L0_xattn_fc_W"], ld["fcW"])
            for m in (0, 1):
                weight(Wo[m], par(m, "Wo"), ld[f"Wo{m}"])
            row(c_row[:], par(0, "bo"), ld["rows"])
            row(bo_v[:], par(1, "bo"), ld["rows"])
            wait(sp, z1_ready, 0, 4, 4)
            load_x(1)

            def body(i, back, front, norms):
                X, Y, Z = i, i + 1, i + 2
                if norms:
                    wait(sp, zc_full, Y, 4, 4)
                    wait(sp, z2r_lo_done, Y, 2, 2)
                    for m in (0, 1):
                        load_ctx(Z, m)
                    if not isinstance(i, int) or i + 3 < PAIRS:
                        wait(sp, z1_ready, Z, 4, 4)
                        load_x(i + 3)
                if not back:
                    sp.wait_ge(WA_full, 4)
                    load_res(0)
                if back:
                    if front:
                        wait(sp, y_ready, X, 4, 4)
                        load_res(Y)
                    for b in (0, 1):
                        if not front and b == 1:
                            for t in range(T):
                                wait(sp, out_ready, X, 4, T + t + 1)
                                sp.dma_start(out_rows[X, :, b, t * D:(t + 1) * D], y[:, T + t, :]).then_inc(stored[b], 16)
                            continue
                        wait(sp, out_ready, X, 4, (b + 1) * T)
                        sp.dma_start(out_rows[X, :, b, :],
                                     y[:, b * T:(b + 1) * T, :].rearrange("p t d -> p (t d)")).then_inc(stored[b], 16)

            body(-1, False, True, True)
            body(0, True, True, True)
            with sp.Fori(1, PAIRS - 3) as i:
                body(i, True, True, True)
            body(PAIRS - 3, True, True, True)
            body(PAIRS - 2, True, True, False)
            body(PAIRS - 1, True, False, False)
            sp.wait_ge(stored[0], 16 * PAIRS)
            sp.wait_ge(stored[1], 16 * (PAIRS - 1 + T))

        @block.tensor
        def _(pe):
            def mm(out, l, r, start, stop):
                return nc.tensor.matmul(out, l, r, start=start, stop=stop)

            pe.wait_ge(ld["vec"], 16)
            pe.wait_ge(ident_ready, 1)
            nc.tensor.transpose(turn[3][:, 0:NVEC], vec_rows[0:NVEC, :], ident[0:NVEC, 0:NVEC]).then_inc(vec_turned, 1)
            for m in (0, 1):
                pe.wait_ge(ld[f"WkT{m}"], 16)
                for j in range(DC):
                    k = m * DC + j
                    if j % 2 == 0 and j // 2 < len(ld[f"WqT{m}"]):
                        pe.wait_ge(ld[f"WqT{m}"][j // 2], 16)
                    if k >= 4:
                        pe.wait_ge(M_scaled_done, k - 3)
                        pe.wait_ge(w_dots, k - 3)
                    for e in range(EC):
                        last = mm(prod[k % 4][:, 0:D2 + 1], WqT[m][:, e, j * P:(j + 1) * P], WkT[m][:, e, :],
                                  e == 0, e == EC - 1)
                    last.then_inc(M_full, 1)
            pe.wait_ge(vec_ready, 1)
            pe.wait_ge(ones_ready, 1)

            def key_term(m):
                pe.wait_ge(M_scaled_done, DC + 3 + m)
                pe.wait_ge(w_dots, DC + 3 + m)
                pe.wait_ge(bq_cols, m + 1)
                for j in range(D2C):
                    for e in range(EC):
                        last = mm(prod[2 + m][:, j:j + 1], WkT[m][:, e, j * P:(j + 1) * P], col(BQ, m, e, e + 1),
                                  e == 0, e == EC - 1)
                last.then_inc(u_full, 1)

            for m in (0, 1):
                pe.wait_ge(diag_ready, m + 1)
                for j in range(DC):
                    last = mm(turn[2 + m][:, j * P:(j + 1) * P], ones[:], w_diag[:, m, j, :], True, True)
                last.then_inc(w_full, 1)
                if m == 0:
                    key_term(0)

            def row_terms():
                pe.wait_ge(r0_parts, 5)
                mm(prod[3][:, D2C:D2C + 2], ones[:], r0_cols, True, True).then_inc(r0_full, 1)

            def output_weights():
                for m in (0, 1):
                    pe.wait_ge(ld[f"WvT{m}"], 16)
                    pe.wait_ge(ld[f"Wo{m}"], 16)
                    for j in range(D2C):
                        k = m * D2C + j
                        wait(pe, zc_lo, 0, 4, k + 1)
                        for e in range(EC):
                            last = mm(turn[k][:], WvT[m][:, e, j * P:(j + 1) * P], Wo[m][:, e, :], e == 0, e == EC - 1)
                        last.then_inc(WA_full, 1)

            def constant_rows():
                wait(pe, exp_done, 0, 8, 2)
                pe.wait_ge(row_sums, 2 * EC)
                mm(prod[0][:], ones[:], c_row[:], True, True).then_inc(rows_full, 1)
                wait(pe, exp_done, 0, 8, 4)
                pe.wait_ge(f_parts, 2)
                mm(prod[1][:], ones[:], f_row[:], True, False)
                mm(prod[1][:], ones[:], fcW_b[:, 0, :], False, False)
                mm(prod[1][:], ones[:], fcW_b[:, 1, :], False, True).then_inc(rows_full, 1)

            def body(i, back, front, norms):
                X, Y = i, i + 1

                def turn_z1(k):
                    if k == 0 and back:
                        wait(pe, z1_ready, Y, 4, 4)
                    if not back and k >= 2:
                        pe.wait_ge(w_ready, k - 1)
                    wait(pe, pt_lo, X, 4, k + 1)
                    for n in range(TILES):
                        if k == 0 and not back:
                            pe.wait_ge(z1_ready, n + 1)
                        last = nc.tensor.transpose(turn[k][:, n * P:(n + 1) * P], z1[:, n, k * P:(k + 1) * P], ident[:])
                    last.then_inc(zx_full, 1)

                def context(k):
                    b, m = divmod(k, 2)
                    wait(pe, pt_lo, X, 4, k + 1)
                    wait(pe, out_ready, X - 1, 4, k + 1)
                    if isinstance(i, int) and i == 0 and k < 2:
                        pe.wait_ge(rows_ready, k + 1)
                    if b == 0:
                        wait(pe, z2r_lo_done, X, 2, m + 1)
                    for j in range(D2C):
                        for kt in range(T):
                            l = (z2r_hi[:, m, b * T + kt, j * P:(j + 1) * P], z2r_lo[:, m, b * T + kt, j * P:(j + 1) * P])
                            r = (share_hi[:, k, kt * S:(kt + 1) * S], share_lo[:, k, kt * S:(kt + 1) * S])
                            for q, (ll, rr) in enumerate(passes(*l, *r)):
                                last = mm(prod[k][:, j * S:(j + 1) * S], ll, rr, kt == 0 and q == 0,
                                          kt == T - 1 and q == 2)
                    last.then_inc(c_full, 1)

                def project(k):
                    m, j = divmod(k, D2C)
                    if back:
                        wait(pe, c_lo, X, 4, k + 1)
                    elif k < 2:
                        pe.wait_ge(M_lo_done[0], DC)
                    else:
                        pe.wait_ge(M_lo_done[1], DC)
                        pe.wait_ge(u_ready, k - 1)
                        if k == 3:
                            pe.wait_ge(r0_ready, 1)
                    for c in range(DC):
                        if k == 0:
                            wait(pe, zx_lo, Y, 4, c + 1)
                        l = (M_hi[:, m, c, j * P:(j + 1) * P], M_lo[:, m, c, j * P:(j + 1) * P])
                        for q, (ll, rr) in enumerate(passes(*l, z1T_hi[:, c, :], z1T_lo[:, c, :])):
                            last = mm(prod[k][:], ll, rr, c == 0 and q == 0, c == DC - 1 and q == 2)
                    last.then_inc(t_full, 1)

                def turn_z2(k):
                    m, j = divmod(k, D2C)
                    wait(pe, z2_ready, Y, 8, 4 * m + 4)
                    wait(pe, zx_lo, Y, 4, k + 1)
                    for n in range(TILES):
                        last = nc.tensor.transpose(turn[k][:, n * P:(n + 1) * P], z2[:, m, n, j * P:(j + 1) * P], ident[:])
                    last.then_inc(zc_full, 1)

                def output(n):
                    b, t = divmod(n, T)
                    if t == 0:
                        wait(pe, c_lo, X, 4, 2 * b + 2)
                    if front:
                        wait(pe, t_lo, Y, 4, n + 1)
                    if isinstance(i, int) and (i, n) == (0, 0):
                        pe.wait_ge(WA_lo_done, 4)
                    for m in (0, 1):
                        for j in range(D2C):
                            l = (cT_hi[:, b, m, j, t * P:(t + 1) * P], cT_lo[:, b, m, j, t * P:(t + 1) * P])
                            for q, (ll, rr) in enumerate(passes(*l, WA_hi[:, m, j, :], WA_lo[:, m, j, :])):
                                last = mm(prod[n][:], ll, rr, (m, j, q) == (0, 0, 0), (m, j, q) == (1, D2C - 1, 2))
                    last.then_inc(f_full, 1)

                def scores(k):
                    b, m = divmod(k, 2)
                    if k < 2:
                        wait(pe, t_lo, Y, 4, 2 * m + 2)
                        wait(pe, zc_lo, Y, 4, 2 * m + 2)
                    if back:
                        wait(pe, y_ready, X, 4, k + 1)
                    for t in range(T):
                        n = b * T + t
                        for j in range(D2C):
                            l = (tT_hi[:, m, j, n * P:(n + 1) * P], tT_lo[:, m, j, n * P:(n + 1) * P])
                            r = (z2T_hi[:, m, j, b * S:(b + 1) * S], z2T_lo[:, m, j, b * S:(b + 1) * S])
                            for q, (ll, rr) in enumerate(passes(*l, *r)):
                                last = mm(prod[k][:, t * S:(t + 1) * S], ll, rr, j == 0 and q == 0,
                                          j == D2C - 1 and q == 2)
                    last.then_inc(s_full, 1)

                def turn_y(n):
                    wait(pe, yn_ready, X, 4, n + 1)
                    if front:
                        wait(pe, zc_lo, Y, 4, n + 1)
                    for c in range(DC):
                        last = nc.tensor.transpose(turn[n][:, c * P:(c + 1) * P], yn[:, n % 2, c * P:(c + 1) * P], ident[:])
                    last.then_inc(yt_full, 1)

                def linear(n):
                    wait(pe, yt_lo, X, 4, n + 1)
                    if front:
                        wait(pe, exp_done, Y, 8, 2 * n + 2)
                    for c in range(DC):
                        l = (share_hi[:, n, c * P:(c + 1) * P], share_lo[:, n, c * P:(c + 1) * P])
                        for q, (ll, rr) in enumerate(passes(*l, fc_hi[:, c, :], fc_lo[:, c, :])):
                            last = mm(prod[n][:], ll, rr, c == 0 and q == 0, c == DC - 1 and q == 2)
                    last.then_inc(h_full, 1)

                def turn_probs(k):
                    b, m = divmod(k, 2)
                    wait(pe, probs_ready, Y, 8, 2 * k + 2)
                    if back:
                        wait(pe, yt_lo, X, 4, k + 1)
                    else:
                        pe.wait_ge(WA_scaled, k + 1)
                        pe.wait_ge(row_sums, 2 * EC)
                    for kt in range(T):
                        for t in range(T):
                            last = nc.tensor.transpose(turn[k][:, kt * S + t * P:kt * S + (t + 1) * P],
                                                       probs[:, b, m, t, kt * P:(kt + 1) * P], ident[:])
                    last.then_inc(pt_full, 1)

                for k in range(4):
                    if front:
                        turn_z1(k)
                    if back:
                        context(k)
                if front:
                    for k in range(4):
                        project(k)
                        turn_z2(k)
                        if not back and k == 0:
                            key_term(1)
                        if not back and k == 1:
                            row_terms()
                for n in range(4):
                    if back:
                        output(n)
                        if n >= 2:
                            turn_y(n - 2)
                if not front:
                    linear(0)
                for k in range(4):
                    if front:
                        scores(k)
                    if back and k in (1, 2):
                        turn_y(k + 1)
                if not back:
                    output_weights()
                for n in range(4):
                    if back:
                        if isinstance(i, int) and (i, n) == (0, 0):
                            pe.wait_ge(fc_lo_done, DC)
                        if front or n > 0:
                            linear(n)
                    if front and n > 0:
                        turn_probs(n - 1)
                if front:
                    turn_probs(3)
                if not back:
                    constant_rows()

            steps(body)(pe)

        @block.scalar
        def _(act):
            def hi(out, in_, **kw):
                return nc.scalar.activation(out, in_, ACT.Identity if "bias" in kw else ACT.Copy, **kw)

            def hi_M(m, j):
                act.wait_ge(M_scaled_done, m * DC + j + 1)
                hi(M_hi[:, m, j, :], M_scaled[:, m, j, :]).then_inc(M_hi_done, 1)

            def sum_products(m):
                act.wait_ge(products, m + 1)
                for e in range(EC):
                    nc.scalar.activation(WqT_b1[m][:, e, :], WqT_b1[m][:, e, :], ACT.Copy,
                                         accum_out=col(BQ, m, e, e + 1)).then_inc(sums, 1)

            def diagonals(m):
                for j in range(DC):
                    act.wait_ge(w_dots, m * DC + j + 1)
                    last = hi(w_diag[:, m, j, :], ident[:], scale=col(W, m, j, j + 1))
                last.then_inc(diag_ready, 1)

            act.wait_ge(ident_ready, 1)
            hi_M(0, 0)
            hi_M(0, 1)
            sum_products(0)
            hi_M(0, 2)
            hi_M(0, 3)
            diagonals(0)
            for j in range(DC):
                hi_M(1, j)
            diagonals(1)

            def hi_fc():
                act.wait_ge(ld["fcW"], 16)
                for c in range(DC):
                    hi(fc_hi[:, c, :], fcW[:, c, :], scale=vec_cols("ln_g")[:, c:c + 1]).then_inc(fc_hi_done, 1)

            def hi_WA():
                for m in (0, 1):
                    for j in range(D2C):
                        k = m * D2C + j
                        act.wait_ge(WA_full, k + 1)
                        if k >= 2:
                            act.wait_ge(WA_lo_done, k - 1)
                        hi(WA_f32[:, k % 2, :], turn[k][:],
                           scale=vec_cols((m, "ln2_g"))[:, j:j + 1]).then_inc(WA_scaled, 1)
                        act.wait_ge(WA_scaled, k + 1)
                        hi(WA_hi[:, m, j, :], WA_f32[:, k % 2, :]).then_inc(WA_hi_done, 1)

            def rows_c_f():
                for k, row in enumerate((c_row, f_row)):
                    act.wait_ge(rows_full, k + 1)
                    nc.scalar.activation(row[:], prod[k][:], ACT.Copy).then_inc(rows_ready, 1)

            def body(i, back, front, norms):
                X, Y = i, i + 1

                def sum_product(k):
                    n, m = divmod(k, 2)
                    slot = probs[:, k % 4 // 2, k % 2, :, :].rearrange("p t s -> p (t s)")
                    wait(act, r_product, Y, 8, k + 1)
                    nc.scalar.activation(slot, slot, ACT.Copy, accum_out=r_sum[:, n, m:m + 1]).then_inc(r_summed, 1)

                def hi_y(n):
                    wait(act, yt_full, X, 4, n + 1)
                    hi(share_hi[:, n, :], turn[n][:]).then_inc(yt_hi, 1)

                def exp(k):
                    b, m = divmod(k, 2)
                    wait(act, bias_ready, Y, 4, k + 1)
                    for t in range(T):
                        nc.scalar.activation(probs[:, b, m, t, :], prod[k][:, t * S:(t + 1) * S], ACT.Exp,
                                             bias=exp_bias[:, b, m, t:t + 1],
                                             accum_out=exp_sum[:, b, m, t:t + 1]).then_inc(exp_done, 1)

                def normalise(k):
                    b, m = divmod(k, 2)
                    wait(act, inv_ready, Y, 4, k + 1)
                    for t in range(T):
                        nc.scalar.activation(probs[:, b, m, t, :], probs[:, b, m, t, :], ACT.Copy,
                                             scale=exp_inv[:, b, m, t:t + 1]).then_inc(probs_ready, 1)

                for k in range(4):
                    if front:
                        wait(act, zx_full, Y, 4, k + 1)
                        hi(z1T_hi[:, k, :], turn[k][:]).then_inc(zx_hi, 1)
                    if back:
                        b, m = divmod(k, 2)
                        wait(act, c_full, X, 4, k + 1)
                        hi(cT_hi[:, b, m, :, :].rearrange("p j s -> p (j s)"), prod[k][:]).then_inc(c_hi, 1)
                    if back and front and k >= 2:
                        sum_product(2 * k - 4)
                        sum_product(2 * k - 3)
                if not back:
                    sum_products(1)
                    for k in range(4):
                        sum_product(k)
                if front:
                    for k in range(4):
                        m, j = divmod(k, D2C)
                        if j == 0:
                            wait(act, z2_ready, Y, 8, 4 * m + 4)
                            hi(z2r_hi[:, m, :, :].rearrange("p n d -> p (n d)"),
                               z2[:, m, :, :].rearrange("p n d -> p (n d)")).then_inc(z2r_hi_done, 1)
                        wait(act, t_full, Y, 4, k + 1)
                        hi(tT_hi[:, m, j, :], prod[k][:], bias=u_col[:, m, j:j + 1]).then_inc(t_hi, 1)
                        wait(act, zc_full, Y, 4, k + 1)
                        hi(z2T_hi[:, m, j, :], turn[k][:]).then_inc(zc_hi, 1)
                        sum_product(k + 4)
                if back:
                    for n in range(3):
                        hi_y(n)
                if not back:
                    hi_fc()
                if front:
                    exp(0)
                if back:
                    hi_y(3)
                if front:
                    exp(1)
                    normalise(0)
                    exp(2)
                    normalise(1)
                    exp(3)
                    normalise(2)
                    normalise(3)
                    if not back:
                        hi_WA()
                    for k in range(4):
                        wait(act, pt_full, Y, 4, k + 1)
                        hi(share_hi[:, k, :], turn[k][:]).then_inc(pt_hi, 1)
                    if not back:
                        rows_c_f()

            steps(body)(act)

        @block.vector
        def _(dve):
            def lo(out, in_, h):
                return nc.vector.tensor_tensor(out, in_, h.bitcast(F32), ALU.subtract)

            def lo_scaled(out, in_, s, h):
                return nc.vector.scalar_tensor_tensor(out, in_, s, h.bitcast(F32), ALU.mult, ALU.subtract)

            def x_bn_stats(p):
                wait(dve, x_loaded, p, 32, 32)
                for n in range(TILES):
                    nc.vector.bn_stats(x_bn[:, n, :], x_in[:, n, :]).then_inc(x_bn_done, 1)

            def x_bn_wait(p):
                wait(dve, x_bn_done, p, 4, 4)

            def x_bn_aggr():
                for n in range(TILES):
                    nc.vector.bn_aggr(x_mv[:, n, :], x_bn[:, n, :]).then_inc(x_stats, 1)

            def norm_x(p, n):
                wait(dve, x_rstd_done, p, 1, 1)
                nc.vector.tensor_scalar(z1[:, n, :], x_in[:, n, :], x_mv[:, n, 0:1], x_rstd[:, n:n + 1],
                                        ALU.subtract, ALU.mult).then_inc(z1_ready, 1)

            def ctx_bn_stats(p, m):
                wait(dve, ctx_loaded[m], p, 16, 16)
                for n in range(TILES):
                    nc.vector.bn_stats(ctx_bn[:, m, n, :], z2[:, m, n, :]).then_inc(ctx_bn_done, 1)

            def ctx_bn_wait(p, m):
                wait(dve, ctx_bn_done, p, 8, 4 * m + 4)

            def ctx_bn_aggr(m):
                for n in range(TILES):
                    nc.vector.bn_aggr(ctx_mv[:, m, n, :], ctx_bn[:, m, n, :]).then_inc(ctx_stats, 1)

            def norm_ctx(p, m):
                wait(dve, ctx_rstd_done, p, 2, m + 1)
                for n in range(TILES):
                    nc.vector.tensor_scalar(z2[:, m, n, :], z2[:, m, n, :], ctx_mv[:, m, n, 0:1],
                                            ctx_rstd[:, m, n:n + 1], ALU.subtract, ALU.mult).then_inc(z2_ready, 1)

            nc.vector.memset(ones[:], 1.0).then_inc(ones_ready, 1)
            dve.wait_ge(vec_turned, 1)
            nc.vector.tensor_copy(vec[:, 0:NVEC], turn[3][:, 0:NVEC]).then_inc(vec_ready, 1)
            dve.wait_ge(vec_ready, 1)
            for m in (0, 1):
                nc.vector.tensor_scalar(col(G1S, m), vec_cols((m, "ln1_g")), SCALE, None, ALU.mult).then_inc(g1s_ready, 1)
            dve.wait_ge(g1s_ready, 2)

            def lo_M(j):
                dve.wait_ge(M_hi_done, DC + j + 1)
                lo(M_lo[:, 1, j, :], M_scaled[:, 1, j, :], M_hi[:, 1, j, :]).then_inc(M_lo_done[1], 1)

            for k in range(2 * DC):
                m, j = divmod(k, DC)
                dve.wait_ge(ld[f"norm_rows{m}"], 16)
                dve.wait_ge(M_full, k + 1)
                nc.vector.scalar_tensor_tensor(M_scaled[:, m, j, :], prod[k % 4][:, 0:D2], col(G1S, m, j, j + 1),
                                               g2_row[m], ALU.mult, ALU.mult).then_inc(M_scaled_done, 1)
                if k > 0:
                    dve.wait_ge(w_dots, k)
                nc.vector.tensor_tensor_reduce(w_scratch[:], prod[k % 4][:, 0:D2 + 1], b2_one_row[m], 1.0, 0.0, ALU.mult,
                                               ALU.add, col(W, m, j, j + 1)).then_inc(w_dots, 1)
                if k == 3:
                    x_bn_stats(0)
                    x_bn_wait(0)
                    x_bn_aggr()

            def w_rows(m):
                dve.wait_ge(w_full, m + 1)
                nc.vector.scalar_tensor_tensor(w_row[:, m, :], turn[2 + m][:], SCALE, g1_row[m], ALU.mult,
                                               ALU.mult).then_inc(w_ready, 1)

            w_rows(0)
            for n in range(TILES):
                norm_x(0, n)
            w_rows(1)
            ctx_bn_stats(0, 0)
            ctx_bn_wait(0, 0)
            ctx_bn_aggr(0)
            dve.wait_ge(w_ready, 2)
            dve.wait_ge(products, 2)

            def key_term(m):
                dve.wait_ge(u_full, m + 1)
                nc.vector.scalar_tensor_tensor(u_col[:, m, :], prod[2 + m][:, 0:D2C], SCALE, vec_cols((m, "ln2_g")),
                                               ALU.mult, ALU.mult).then_inc(u_ready, 1)
                nc.vector.tensor_tensor_reduce(r0_scratch[:, m, 0:D2C], prod[2 + m][:, 0:D2C], vec_cols((m, "ln2_b")),
                                               1.0, 0.0, ALU.mult, ALU.add, u_b2[:, m:m + 1]).then_inc(r0_parts, 1)
                nc.vector.tensor_tensor_reduce(r0_scratch[:, m, D2C:D2C + EC], col(BQ, m), vec_cols((m, "bk")),
                                               1.0, 0.0, ALU.mult, ALU.add, r0_cols[:, m:m + 1]).then_inc(r0_parts, 1)

            def row_parts():
                dve.wait_ge(r0_parts, 4)
                nc.vector.tensor_tensor(r0_cols, r0_cols, u_b2, ALU.add).then_inc(r0_parts, 1)

            def row_terms():
                dve.wait_ge(r0_full, 1)
                for n in range(TILES):
                    last = nc.vector.tensor_scalar(r0[:, n, :], prod[3][:, D2C:D2C + 2], SCALE, None, ALU.mult)
                last.then_inc(r0_ready, 1)

            def value_bias(k):
                m, half = divmod(k, 2)
                if k == 0:
                    dve.wait_ge(ld["b2_rows"], 32)
                if half == 0:
                    dve.wait_ge(ld[f"WvT{m}"], 16)
                for e in (2 * half, 2 * half + 1):
                    if m + e:
                        dve.wait_ge(dots, m * EC + e)
                    nc.vector.tensor_tensor_reduce(scratch[:], WvT[m][:, e, :], b2_rows[:, m, :], 1.0, 0.0, ALU.mult,
                                                   ALU.add, col(BV, m, e, e + 1)).then_inc(dots, 1)
                if half:
                    dve.wait_ge(dots, (m + 1) * EC)
                    nc.vector.tensor_tensor(col(BV, m), col(BV, m), vec_cols((m, "bv")), ALU.add).then_inc(bv_ready, 1)

            def output_row(k):
                m, half = divmod(k, 2)
                if half == 0:
                    dve.wait_ge(ld[f"Wo{m}"], 16)
                    dve.wait_ge(bv_ready, m + 1)
                for e in (2 * half, 2 * half + 1):
                    if m + e == 0:
                        dve.wait_ge(rows_begun, 3)
                    else:
                        dve.wait_ge(row_sums, m * EC + e)
                    nc.vector.scalar_tensor_tensor(c_row[:], Wo[m][:, e, :], col(BV, m, e, e + 1), c_row[:], ALU.mult,
                                                   ALU.add).then_inc(row_sums, 1)

            def lo_fc(c):
                dve.wait_ge(fc_hi_done, c + 1)
                lo_scaled(fc_lo[:, c, :], fcW[:, c, :], vec_cols("ln_g")[:, c:c + 1], fc_hi[:, c, :]).then_inc(fc_lo_done, 1)

            def body(i, back, front, norms):
                X, Y, Z = i, i + 1, i + 2
                for k in range(4):
                    if front:
                        wait(dve, zx_hi, Y, 4, k + 1)
                        lo(z1T_lo[:, k, :], turn[k][:], z1T_hi[:, k, :]).then_inc(zx_lo, 1)
                    if back:
                        b, m = divmod(k, 2)
                        wait(dve, c_hi, X, 4, k + 1)
                        lo(cT_lo[:, b, m, :, :].rearrange("p j s -> p (j s)"), prod[k][:],
                           cT_hi[:, b, m, :, :].rearrange("p j s -> p (j s)")).then_inc(c_lo, 1)
                if not back:
                    key_term(0)
                    norm_ctx(0, 0)
                    ctx_bn_stats(0, 1)
                    ctx_bn_wait(0, 1)
                    ctx_bn_aggr(1)
                    for j in range(DC):
                        lo_M(j)
                    dve.wait_ge(M_lo_done[1], DC)
                    norm_ctx(0, 1)
                    key_term(1)
                    row_parts()
                if norms and back:
                    x_bn_stats(Z)
                if front:
                    for k in range(4):
                        m, j = divmod(k, D2C)
                        wait(dve, t_hi, Y, 4, k + 1)
                        if norms and back and k == 0:
                            x_bn_wait(Z)
                        nc.vector.scalar_tensor_tensor(tT_lo[:, m, j, :], prod[k][:], u_col[:, m, j:j + 1],
                                                       tT_hi[:, m, j, :].bitcast(F32), ALU.add,
                                                       ALU.subtract).then_inc(t_lo, 1)
                        if norms and back and k == 0:
                            x_bn_aggr()
                        wait(dve, zc_hi, Y, 4, k + 1)
                        lo(z2T_lo[:, m, j, :], turn[k][:], z2T_hi[:, m, j, :]).then_inc(zc_lo, 1)
                        if isinstance(i, int) and i == 0:
                            lo_fc(k)
                        if not back and k == 1:
                            row_terms()
                if isinstance(i, int) and i == 0:
                    dve.wait_ge(fc_lo_done, DC)

                def norm_x_tiles(n0, n1):
                    wait(dve, r_product, Y, 8, 8)
                    for n in range(n0, n1):
                        norm_x(Z, n)

                if norms and back:
                    norm_x_tiles(0, TILES - 2)

                def norm_y(n):
                    wait(dve, y_rstd_done, X, 4, n + 1)
                    if n >= 2:
                        wait(dve, yt_full, X, 4, n - 1)
                    nc.vector.tensor_scalar(yn[:, n % 2, :], y[:, n, :], y_mv[:, n, 0:1], y_rstd[:, n:n + 1],
                                            ALU.subtract, ALU.mult).then_inc(yn_ready, 1)

                def lo_y(n):
                    wait(dve, yt_hi, X, 4, n + 1)
                    lo(share_lo[:, n, :], turn[n][:], share_hi[:, n, :]).then_inc(yt_lo, 1)

                def invert(k):
                    b, m = divmod(k, 2)
                    wait(dve, exp_done, Y, 8, 2 * k + 2)
                    nc.vector.reciprocal(exp_inv[:, b, m, :], exp_sum[:, b, m, :]).then_inc(inv_ready, 1)

                def row_max(k):
                    b, m = divmod(k, 2)
                    wait(dve, s_full, Y, 4, k + 1)
                    nc.vector.tensor_reduce(neg_max[:, b, m, :], prod[k][:].rearrange("p (t s) -> p t s", t=T),
                                            AX_X, ALU.max, negate=True).then_inc(max_ready, 1)

                if back:
                    for n in range(4):
                        wait(dve, f_full, X, 4, n + 1)
                        wait(dve, res_ready, X, 4, n + 1)
                        wait(dve, stored[n // T], X - 1, 16, 16)
                        nc.vector.tensor_tensor(y[:, n, :], prod[n][:], x_res[:, n, :], ALU.add).then_inc(y_ready, 1)
                        if n > 0:
                            norm_y(n - 1)
                        wait(dve, y_ready, X, 4, n + 1)
                        nc.vector.bn_stats(y_bn[:, n, :], y[:, n, :]).then_inc(y_bn_done, 1)
                        wait(dve, y_bn_done, X, 4, n + 1)
                        if n >= 2:
                            lo_y(n - 2)
                        elif norms:
                            norm_x(Z, TILES - 2 + n)
                        nc.vector.bn_aggr(y_mv[:, n, :], y_bn[:, n, :]).then_inc(y_stats, 1)
                if front:
                    row_max(0)
                if back:
                    norm_y(3)
                    lo_y(2)
                if front:
                    row_max(1)
                if back:
                    lo_y(3)
                if not back:
                    value_bias(0)
                    row_max(2)
                    invert(0)
                    row_max(3)
                    invert(1)
                    value_bias(1)
                    invert(2)
                    output_row(0)
                    invert(3)
                    output_row(1)
                    for k in (2, 3):
                        value_bias(k)
                    for k in (2, 3):
                        output_row(k)
                    x_bn_stats(1)
                    x_bn_wait(1)
                    x_bn_aggr()
                    for m in (0, 1):
                        ctx_bn_stats(1, m)
                        ctx_bn_wait(1, m)
                        ctx_bn_aggr(m)
                    norm_x_tiles(0, TILES)
                elif front:
                    invert(0)
                    row_max(2)
                    invert(1)
                    row_max(3)
                for n in range(4):
                    if norms and back and n < 2:
                        ctx_bn_stats(Z, n)
                        ctx_bn_wait(Z, n)
                    if front and back and n < 2:
                        invert(n + 2)
                    if back:
                        wait(dve, h_full, X, 4, n + 1)
                        wait(dve, yf_ready, X, 4, n + 1)
                        nc.vector.tensor_tensor(y[:, n, :], prod[n][:], y[:, n, :], ALU.add).then_inc(out_ready, 1)
                    if norms:
                        if n >= 2:
                            norm_ctx(Z, n - 2)
                        elif back:
                            ctx_bn_aggr(n)
                    if front and n > 0:
                        wait(dve, pt_hi, Y, 4, n)
                        lo(share_lo[:, n - 1, :], turn[n - 1][:], share_hi[:, n - 1, :]).then_inc(pt_lo, 1)
                if front:
                    wait(dve, pt_hi, Y, 4, 4)
                    lo(share_lo[:, 3, :], turn[3][:], share_hi[:, 3, :]).then_inc(pt_lo, 1)

            steps(body)(dve)

        @block.gpsimd
        def _(pool):
            nc.gpsimd.memset(ident[:], 0.0).then_inc(zeroed, 1)
            pool.wait_ge(zeroed, 1)
            nc.gpsimd.affine_select(out=ident[:], in_=ident[:], compare_op=ALU.not_equal, fill=1.0, base=0,
                                    pattern=[[-1, P]], channel_multiplier=1).then_inc(ident_ready, 1)
            nc.gpsimd.memset(minus_half[:], -0.5).then_inc(zeroed, 1)
            nc.gpsimd.memset(eps[:], EPS).then_inc(zeroed, 1)
            nc.gpsimd.memset(one_128th[:], 1.0 / P).then_inc(zeroed, 1)
            pool.wait_ge(zeroed, 4)

            def rstd(ve, out, mv, width, stats, stats_at, ve_done, ve_at, done):
                wait(pool, stats, *stats_at)
                nc.gpsimd.tensor_tensor(ve, mv, eps[:, 0:width], ALU.add).then_inc(ve_done, 1)
                wait(pool, ve_done, *ve_at)
                nc.gpsimd.tensor_tensor(out, ve, minus_half[:, 0:width], ALU.pow).then_inc(done, 1)

            def rstd_x(p):
                rstd(x_ve[:], x_rstd[:], x_mv[:, :, 1], TILES, x_stats, (p, 4, 4), x_ve_done, (p, 1, 1), x_rstd_done)

            def rstd_ctx(p, m):
                rstd(ctx_ve[:, m, :], ctx_rstd[:, m, :], ctx_mv[:, m, :, 1], TILES, ctx_stats, (p, 8, 4 * m + 4),
                     ctx_ve_done, (p, 2, m + 1), ctx_rstd_done)

            def product(m):
                pool.wait_ge(ld[f"norm_rows{m}"], 16)
                for loaded in ld[f"WqT{m}"]:
                    pool.wait_ge(loaded, 16)
                if m:
                    pool.wait_ge(M_full, 2 * DC)
                nc.gpsimd.tensor_tensor(WqT_b1[m][:], WqT[m][:], b1_row[m][:, None, :].to_broadcast([P, EC, D]),
                                        ALU.mult).then_inc(products, 1)

            def bq_column(m):
                pool.wait_ge(sums, (m + 1) * EC)
                nc.gpsimd.tensor_tensor(col(BQ, m), col(BQ, m), vec_cols((m, "bq")), ALU.add).then_inc(bq_cols, 1)

            def lo_M(j):
                pool.wait_ge(M_hi_done, j + 1)
                nc.gpsimd.tensor_tensor(M_lo[:, 0, j, :], M_scaled[:, 0, j, :], M_hi[:, 0, j, :].bitcast(F32),
                                        ALU.subtract).then_inc(M_lo_done[0], 1)

            pool.wait_ge(vec_ready, 1)
            product(0)
            for j in range(DC):
                lo_M(j)
            bq_column(0)
            rstd_x(0)
            product(1)
            pool.wait_ge(w_ready, 2)

            def linear_row_products():
                pool.wait_ge(ld["fcW"], 16)
                nc.gpsimd.tensor_tensor(fcW_b[:], fcW[:], vec_cols("ln_b")[:, :, None].to_broadcast([P, DC, D]),
                                        ALU.mult).then_inc(f_parts, 1)

            def linear_row_sum():
                pool.wait_ge(f_parts, 1)
                nc.gpsimd.tensor_tensor(fcW_b[:, 0:2, :], fcW_b[:, 0:2, :], fcW_b[:, 2:4, :], ALU.add).then_inc(f_parts, 1)

            def lo_WA(k):
                m, j = divmod(k, D2C)
                pool.wait_ge(WA_hi_done, k + 1)
                nc.gpsimd.tensor_tensor(WA_lo[:, m, j, :], WA_f32[:, k % 2, :], WA_hi[:, m, j, :].bitcast(F32),
                                        ALU.subtract).then_inc(WA_lo_done, 1)

            def body(i, back, front, norms):
                X, Y, Z = i, i + 1, i + 2
                if front:
                    wait(pool, z1_ready, Y, 4, 4)
                    for k in range(2 * TILES):
                        n, m = divmod(k, 2)
                        if k < 4:
                            wait(pool, pt_full, X, 4, k + 1)
                        else:
                            wait(pool, r_summed, Y, 8, k - 3)
                        nc.gpsimd.tensor_tensor(probs[:, k % 4 // 2, k % 2, :, :].rearrange("p t s -> p (t s)"),
                                                z1[:, n, :], w_row[:, m, :], ALU.mult).then_inc(r_product, 1)
                        if not back and k in (1, 3):
                            rstd_ctx(0, k // 2)
                        if not back and k == 1:
                            bq_column(1)
                if back:
                    wait(pool, res_loaded, X, 32, 32)
                    if isinstance(i, int) and i == 0:
                        pool.wait_ge(rows_ready, 1)
                    for n in range(TILES):
                        nc.gpsimd.tensor_tensor(x_res[:, n, :], x_res[:, n, :], c_row[:], ALU.add).then_inc(res_ready, 1)
                if norms and back:
                    rstd_x(Z)
                if not back:
                    pool.wait_ge(ld["fc_b"], 16)
                    pool.wait_ge(ld["rows"], 32)
                    nc.gpsimd.tensor_tensor(c_row[:], c_row[:], bo_v[:], ALU.add).then_inc(rows_begun, 1)
                    nc.gpsimd.tensor_tensor(f_row[:], f_row[:], one_128th[:].to_broadcast([P, D]),
                                            ALU.mult).then_inc(rows_begun, 1)
                    pool.wait_ge(rows_begun, 2)
                    nc.gpsimd.tensor_tensor(c_row[:], c_row[:], one_128th[:].to_broadcast([P, D]),
                                            ALU.mult).then_inc(rows_begun, 1)

                def lo_z2_rows():
                    for m in (0, 1):
                        wait(pool, z2r_hi_done, Y, 2, m + 1)
                        nc.gpsimd.tensor_tensor(z2r_lo[:, m, :, :].rearrange("p n d -> p (n d)"),
                                                z2[:, m, :, :].rearrange("p n d -> p (n d)"),
                                                z2r_hi[:, m, :, :].rearrange("p n d -> p (n d)").bitcast(F32),
                                                ALU.subtract).then_inc(z2r_lo_done, 1)

                if back and front:
                    lo_z2_rows()
                if back:
                    for n in range(TILES):
                        rstd(y_ve[:, n:n + 1], y_rstd[:, n:n + 1], y_mv[:, n, 1:2], 1, y_stats, (X, 4, n + 1),
                             y_ve_done, (X, 4, n + 1), y_rstd_done)
                if front:
                    wait(pool, r_summed, Y, 8, 8)
                    if not back:
                        pool.wait_ge(r0_ready, 1)
                    nc.gpsimd.tensor_tensor(r_sb[:], r_sum[:], r0[:], ALU.add).then_inc(r_ready, 1)
                    wait(pool, r_ready, Y, 1, 1)
                    for k in range(4):
                        b, m = divmod(k, 2)
                        wait(pool, max_ready, Y, 4, k + 1)
                        r = r_sb[:, b * T:(b + 1) * T, m]
                        nc.gpsimd.tensor_tensor(neg_top[:, b, m, :], neg_max[:, b, m, :], r, ALU.subtract).then_inc(top_ready, 1)
                        wait(pool, top_ready, Y, 4, k + 1)
                        nc.gpsimd.tensor_tensor(exp_bias[:, b, m, :], neg_top[:, b, m, :], r, ALU.add).then_inc(bias_ready, 1)
                if back:
                    if isinstance(i, int) and i == 0:
                        pool.wait_ge(rows_ready, 2)
                    for n in range(TILES):
                        wait(pool, yn_ready, X, 4, n + 1)
                        nc.gpsimd.tensor_tensor(y[:, n, :], y[:, n, :], f_row[:], ALU.add).then_inc(yf_ready, 1)
                if not back:
                    lo_z2_rows()
                    linear_row_products()
                    lo_WA(0)
                    lo_WA(1)
                    linear_row_sum()
                    rstd_x(Z)
                    lo_WA(2)
                    lo_WA(3)
                if norms:
                    for m in (0, 1):
                        rstd_ctx(Z, m)

            steps(body)(pool)


def kernel(**inputs):
    import numpy as _np
    import concourse.bacc as _bacc
    from concourse import mybir as _mybir
    from concourse.bass_utils import run_bass_kernel_spmd as _run

    nc = _bacc.Bacc("TRN2", target_bir_lowering=False, num_devices=1)
    laid = dict(inputs)
    for m, mode in enumerate(MODS):
        for w in ("Wq", "Wk", "Wv"):
            laid[f"{w}T{m}"] = _np.asarray(inputs[f"L0_xattn_{mode}_{w}"]).T
        laid[f"WkT{m}"] = _np.concatenate([laid[f"WkT{m}"], _np.asarray(inputs[f"L0_xattn_{mode}_bk"])[:, None]], axis=1)
    laid["vectors"] = _np.concatenate([_np.asarray(inputs[n]).reshape(-1, P) for _, n in VECTORS])
    laid["norm_rows"] = _np.stack([_np.concatenate(
        [_np.asarray(inputs[f"L0_xattn_{mode}_{n}"]) for n in ("ln1_b", "ln1_g", "ln2_g", "ln2_b")]
        + [_np.ones(1, _np.float32)]) for mode in MODS])
    arrays, aps = {}, {}
    for name, value in laid.items():
        v = _np.ascontiguousarray(value)
        arrays[f"in_{name}_dram"] = v
        aps[name] = nc.dram_tensor(f"in_{name}_dram", v.shape, _mybir.dt.from_np(v.dtype), kind="ExternalInput").ap()
    aps["out"] = nc.dram_tensor("out_0_dram", inputs["x"].shape, _mybir.dt.float32, kind="ExternalOutput").ap()
    build(nc, aps)
    r = _run(nc, [arrays], core_ids=[0])
    return r.results[0]["out_0_dram"]
```
